# Optimizing a Trainium2 kernel written in Bass

```python
import numpy as np
import jax
import jax.numpy as jnp

def _softmax(x, axis=-1):
    return jax.nn.softmax(x, axis=axis)

def _gelu(x):
    return jax.nn.gelu(x, approximate=True)

def _silu(x):
    return jax.nn.silu(x)

def _sigmoid(x):
    return jax.nn.sigmoid(x)

def _layernorm(x, axis=-1, eps=1e-05):
    m = jnp.mean(x, axis=axis, keepdims=True)
    v = jnp.var(x, axis=axis, keepdims=True)
    return (x - m) / jnp.sqrt(v + eps)

def _scatter_add(tgt, idx, src, axis=0):
    return tgt.at[idx].add(src)

def _segment_sum(src, seg, n):
    return jax.ops.segment_sum(src, seg, n)
kernel_name = 'mk_vit_tower_d1_tok_img768_r4_65c7a1'

def setup_inputs(seed: int=0):
    np.random.seed(seed)
    _w = jnp.asarray

    def _rec_inputs():
        import jax
        import jax.numpy as jnp
        _rk = jax.random.key(seed)
        x = -0.000356955 + 1 * jax.random.normal(jax.random.fold_in(_rk, 1), (64, 3, 224, 224), jnp.float32)
        return x
    x = _rec_inputs()

    def _L0_tok_setup():
        import jax, jax.numpy as jnp
        import numpy as np
        N_PATCHES = 14
        HIDDEN_D = 192
        LN_EPS = 1e-05

        def positional_embeddings(seq_len, d):
            i = jnp.arange(seq_len, dtype=jnp.float32)[:, None]
            j = jnp.arange(d, dtype=jnp.float32)[None, :]
            exponent = jnp.floor(j / 2.0) * 2.0 / d
            angle = i / jnp.power(10000.0, exponent)
            return jnp.where(jnp.arange(d)[None, :] % 2 == 0, jnp.sin(angle), jnp.cos(angle))

        def patchify(images, n_patches):
            B, C, H, W = images.shape
            ph, pw = (H // n_patches, W // n_patches)
            x = images.reshape(B, C, n_patches, ph, n_patches, pw)
            x = x.transpose(0, 2, 4, 1, 3, 5)
            return x.reshape(B, n_patches * n_patches, C * ph * pw)
        key = jax.random.key(seed)
        k_img, k_w, k_b, k_cls = jax.random.split(key, 4)
        B, C, H, W = (128, 3, 224, 224)
        lin_in = H // N_PATCHES * (W // N_PATCHES) * C
        bound = 1.0 / np.sqrt(lin_in)
        return {'images': jax.random.normal(k_img, (B, C, H, W), dtype=jnp.float32), 'W': jax.random.uniform(k_w, (HIDDEN_D, lin_in), jnp.float32, -bound, bound), 'b': jax.random.uniform(k_b, (HIDDEN_D,), jnp.float32, -bound, bound), 'class_token': jax.random.uniform(k_cls, (1, HIDDEN_D), jnp.float32), 'gamma': jnp.ones((HIDDEN_D,), jnp.float32), 'beta': jnp.zeros((HIDDEN_D,), jnp.float32)}
    _L0_tok_all = _L0_tok_setup()
    _L0_tok_in = {k: v for k, v in _L0_tok_all.items() if k in ('W', 'b', 'class_token', 'gamma', 'beta')}
    del _L0_tok_all

    def _L0_attn_setup():
        import jax, jax.numpy as jnp
        import numpy as np
        B, T, C, H = (2, 512, 192, 12)
        D = C // H
        ROPE_THETA = 10000.0

        def _rope_sin_cos(T, D, theta):
            inv_freq = 1.0 / theta ** (jnp.arange(0, D, 2, dtype=jnp.float32) / D)
            ang = jnp.arange(T, dtype=jnp.float32)[:, None] * inv_freq[None, :]
            sin = jnp.concatenate([jnp.sin(ang), jnp.sin(ang)], axis=-1)
            cos = jnp.concatenate([jnp.cos(ang), jnp.cos(ang)], axis=-1)
            return (sin, cos)

        def _rotate_half(x):
            h = x.shape[-1] // 2
            return jnp.concatenate([-x[..., h:], x[..., :h]], axis=-1)
        key = jax.random.key(seed)
        k1, k2, k3 = jax.random.split(key, 3)
        x = jax.random.normal(k1, (B, T, C), dtype=jnp.float32)
        w_qkv = jax.random.normal(k2, (3 * C, C), dtype=jnp.float32) * C ** (-0.5)
        w_proj = jax.random.normal(k3, (C, C), dtype=jnp.float32) * C ** (-0.5)
        return {'x': x, 'w_qkv': w_qkv, 'w_proj': w_proj}
    _L0_attn_all = _L0_attn_setup()
    _L0_attn_in = {k: v for k, v in _L0_attn_all.items() if k in ('w_qkv', 'w_proj')}
    del _L0_attn_all

    def _L0_ffn_setup():
        import jax, jax.numpy as jnp
        import numpy as np
        B, S, H, F = (4, 256, 192, 768)
        EC, EU = (4, 4)
        CAP_FACTOR = 1.0

        def _ffn(x, W1, b1, W2, b2):
            return jax.nn.gelu(x @ W1 + b1, approximate=False) @ W2 + b2

        def _expert_mix(h, route, W1, b1, W2, b2, n_exp):
            out = jnp.zeros_like(h)
            for e in range(n_exp):
                m = (route == e).astype(h.dtype)[:, None]
                out = out + m * _ffn(h, W1[e], b1[e], W2[e], b2[e])
            return out

        def _drop_mask(route, pmax, capacity):
            N = route.shape[0]
            order = jnp.lexsort((-jax.lax.stop_gradient(pmax), route))
            rs = route[order]
            starts = jnp.searchsorted(rs, rs, side='left')
            rank_sorted = jnp.arange(N) - starts
            rank = jnp.zeros((N,), jnp.int32).at[order].set(rank_sorted.astype(jnp.int32))
            return rank >= capacity
        key = jax.random.key(seed)
        ks = jax.random.split(key, 8)

        def w(k, shape, s=0.02):
            return jax.random.normal(k, shape, jnp.float32) * s
        return {'hidden_states': jax.random.normal(ks[0], (B, S, H), jnp.float32), 'Wsc': w(ks[1], (H, EC)), 'bsc': jnp.zeros((EC,), jnp.float32), 'W1c': w(ks[2], (EC, H, F)), 'b1c': jnp.zeros((EC, F), jnp.float32), 'W2c': w(ks[3], (EC, F, H)), 'b2c': jnp.zeros((EC, H), jnp.float32), 'Wsu': w(ks[4], (H, EU)), 'bsu': jnp.zeros((EU,), jnp.float32), 'W1u': w(ks[5], (EU, H, F)), 'b1u': jnp.zeros((EU, F), jnp.float32), 'W2u': w(ks[6], (EU, F, H)), 'b2u': jnp.zeros((EU, H), jnp.float32)}
    _L0_ffn_all = _L0_ffn_setup()
    _L0_ffn_in = {k: v for k, v in _L0_ffn_all.items() if k in ('Wsc', 'bsc', 'W1c', 'b1c', 'W2c', 'b2c', 'Wsu', 'bsu', 'W1u', 'b1u', 'W2u', 'b2u')}
    del _L0_ffn_all
    return {'x': x, 'L0_tok_W': _L0_tok_in['W'], 'L0_tok_b': _L0_tok_in['b'], 'L0_tok_class_token': _L0_tok_in['class_token'], 'L0_tok_gamma': _L0_tok_in['gamma'], 'L0_tok_beta': _L0_tok_in['beta'], 'L0_attn_w_qkv': _L0_attn_in['w_qkv'], 'L0_attn_w_proj': _L0_attn_in['w_proj'], 'L0_ffn_Wsc': _L0_ffn_in['Wsc'], 'L0_ffn_bsc': _L0_ffn_in['bsc'], 'L0_ffn_W1c': _L0_ffn_in['W1c'], 'L0_ffn_b1c': _L0_ffn_in['b1c'], 'L0_ffn_W2c': _L0_ffn_in['W2c'], 'L0_ffn_b2c': _L0_ffn_in['b2c'], 'L0_ffn_Wsu': _L0_ffn_in['Wsu'], 'L0_ffn_bsu': _L0_ffn_in['bsu'], 'L0_ffn_W1u': _L0_ffn_in['W1u'], 'L0_ffn_b1u': _L0_ffn_in['b1u'], 'L0_ffn_W2u': _L0_ffn_in['W2u'], 'L0_ffn_b2u': _L0_ffn_in['b2u']}

def reference(x, L0_tok_W, L0_tok_b, L0_tok_class_token, L0_tok_gamma, L0_tok_beta, L0_attn_w_qkv, L0_attn_w_proj, L0_ffn_Wsc, L0_ffn_bsc, L0_ffn_W1c, L0_ffn_b1c, L0_ffn_W2c, L0_ffn_b2c, L0_ffn_Wsu, L0_ffn_bsu, L0_ffn_W1u, L0_ffn_b1u, L0_ffn_W2u, L0_ffn_b2u):
    import jax
    import jax.numpy as jnp

    def _L0_tok_ref(images, W, b, class_token, gamma, beta):
        import jax, jax.numpy as jnp
        import numpy as np
        N_PATCHES = 14
        HIDDEN_D = 192
        LN_EPS = 1e-05

        def positional_embeddings(seq_len, d):
            i = jnp.arange(seq_len, dtype=jnp.float32)[:, None]
            j = jnp.arange(d, dtype=jnp.float32)[None, :]
            exponent = jnp.floor(j / 2.0) * 2.0 / d
            angle = i / jnp.power(10000.0, exponent)
            return jnp.where(jnp.arange(d)[None, :] % 2 == 0, jnp.sin(angle), jnp.cos(angle))

        def patchify(images, n_patches):
            B, C, H, W = images.shape
            ph, pw = (H // n_patches, W // n_patches)
            x = images.reshape(B, C, n_patches, ph, n_patches, pw)
            x = x.transpose(0, 2, 4, 1, 3, 5)
            return x.reshape(B, n_patches * n_patches, C * ph * pw)
        B = images.shape[0]
        patches = patchify(images, N_PATCHES)
        tokens = jnp.einsum('bpi,di->bpd', patches, W) + b
        cls = jnp.broadcast_to(class_token[None, :, :], (B, 1, HIDDEN_D))
        tokens = jnp.concatenate([cls, tokens], axis=1)
        pos = positional_embeddings(N_PATCHES ** 2 + 1, HIDDEN_D)
        out = tokens + pos[None, :, :]
        mean = out.mean(axis=-1, keepdims=True)
        var = out.var(axis=-1, keepdims=True)
        out = (out - mean) / jnp.sqrt(var + LN_EPS)
        return out * gamma + beta

    def _L0_attn_ref(x, w_qkv, w_proj):
        import jax, jax.numpy as jnp
        import numpy as np
        B, T, C, H = (2, 512, 192, 12)
        D = C // H
        ROPE_THETA = 10000.0

        def _rope_sin_cos(T, D, theta):
            inv_freq = 1.0 / theta ** (jnp.arange(0, D, 2, dtype=jnp.float32) / D)
            ang = jnp.arange(T, dtype=jnp.float32)[:, None] * inv_freq[None, :]
            sin = jnp.concatenate([jnp.sin(ang), jnp.sin(ang)], axis=-1)
            cos = jnp.concatenate([jnp.cos(ang), jnp.cos(ang)], axis=-1)
            return (sin, cos)

        def _rotate_half(x):
            h = x.shape[-1] // 2
            return jnp.concatenate([-x[..., h:], x[..., :h]], axis=-1)
        Bx, Tx, Cx = x.shape
        qkv = jnp.einsum('btc,fc->btf', x, w_qkv)
        qkv = qkv.reshape(Bx, Tx, 3, H, D)
        q = jnp.transpose(qkv[:, :, 0], (0, 2, 1, 3))
        k = jnp.transpose(qkv[:, :, 1], (0, 2, 1, 3))
        v = jnp.transpose(qkv[:, :, 2], (0, 2, 1, 3))
        sin, cos = _rope_sin_cos(Tx, D, ROPE_THETA)
        sin = sin[None, None]
        cos = cos[None, None]
        q = q * cos + _rotate_half(q) * sin
        k = k * cos + _rotate_half(k) * sin
        scale = 1.0 / jnp.sqrt(jnp.array(D, dtype=x.dtype))
        scores = jnp.einsum('bhqd,bhkd->bhqk', q, k) * scale
        causal = jnp.tril(jnp.ones((Tx, Tx), dtype=bool))
        scores = jnp.where(causal[None, None], scores, jnp.finfo(scores.dtype).min)
        probs = jax.nn.softmax(scores, axis=-1)
        out = jnp.einsum('bhqk,bhkd->bhqd', probs, v)
        out = jnp.transpose(out, (0, 2, 1, 3)).reshape(Bx, Tx, Cx)
        out = jnp.einsum('btc,fc->btf', out, w_proj)
        return out

    def _L0_ffn_ref(hidden_states, Wsc, bsc, W1c, b1c, W2c, b2c, Wsu, bsu, W1u, b1u, W2u, b2u):
        import jax, jax.numpy as jnp
        import numpy as np
        B, S, H, F = (4, 256, 192, 768)
        EC, EU = (4, 4)
        CAP_FACTOR = 1.0

        def _ffn(x, W1, b1, W2, b2):
            return jax.nn.gelu(x @ W1 + b1, approximate=False) @ W2 + b2

        def _expert_mix(h, route, W1, b1, W2, b2, n_exp):
            out = jnp.zeros_like(h)
            for e in range(n_exp):
                m = (route == e).astype(h.dtype)[:, None]
                out = out + m * _ffn(h, W1[e], b1[e], W2[e], b2[e])
            return out

        def _drop_mask(route, pmax, capacity):
            N = route.shape[0]
            order = jnp.lexsort((-jax.lax.stop_gradient(pmax), route))
            rs = route[order]
            starts = jnp.searchsorted(rs, rs, side='left')
            rank_sorted = jnp.arange(N) - starts
            rank = jnp.zeros((N,), jnp.int32).at[order].set(rank_sorted.astype(jnp.int32))
            return rank >= capacity
        shp = hidden_states.shape
        h = hidden_states.reshape(-1, shp[-1])
        N = h.shape[0]
        capacity = int(CAP_FACTOR * N / EC)
        pc = jax.nn.softmax(h @ Wsc + bsc, axis=-1)
        pmax_c = jnp.max(pc, axis=-1)
        route_c = jnp.argmax(pc, axis=-1)
        dropped = _drop_mask(route_c, pmax_c, capacity)
        scale_c = (pmax_c / jax.lax.stop_gradient(pmax_c))[:, None]
        common = _expert_mix(h, route_c, W1c, b1c, W2c, b2c, EC) * scale_c
        pu = jax.nn.softmax(h @ Wsu + bsu, axis=-1)
        pmax_u = jnp.max(pu, axis=-1)
        route_u = jnp.argmax(pu, axis=-1)
        scale_u = (pmax_u / jax.lax.stop_gradient(pmax_u))[:, None]
        unique = _expert_mix(h, route_u, W1u, b1u, W2u, b2u, EU) * scale_u
        out = common + dropped[:, None].astype(h.dtype) * unique
        return out.reshape(shp)
    h = _L0_tok_ref(x, L0_tok_W, L0_tok_b, L0_tok_class_token, L0_tok_gamma, L0_tok_beta)
    h = h + _L0_attn_ref(_layernorm(h, axis=-1), L0_attn_w_qkv, L0_attn_w_proj)
    h = h + _L0_ffn_ref(_layernorm(h, axis=-1), L0_ffn_Wsc, L0_ffn_bsc, L0_ffn_W1c, L0_ffn_b1c, L0_ffn_W2c, L0_ffn_b2c, L0_ffn_Wsu, L0_ffn_bsu, L0_ffn_W1u, L0_ffn_b1u, L0_ffn_W2u, L0_ffn_b2u)
    return h

_drawn_inputs = setup_inputs


def setup_inputs(seed=0):
    import zlib

    import numpy as np

    out = dict(_drawn_inputs(seed))
    spreads = {'L0_tok_gamma': (1.0, 0.2),
     'L0_tok_beta': (0.0, 0.1),
     'L0_ffn_bsc': (0.0, 0.1),
     'L0_ffn_b1c': (0.0, 0.329),
     'L0_ffn_b2c': (0.0, 0.1),
     'L0_ffn_bsu': (0.0, 0.618),
     'L0_ffn_b1u': (0.0, 0.662),
     'L0_ffn_b2u': (0.0, 0.1)}
    factors = {}
    for name, (base, spread) in spreads.items():
        noise = np.random.default_rng([zlib.crc32(name.encode()), seed]).standard_normal(out[name].shape)
        drawn = base * np.exp(spread * noise) if base else spread * noise
        out[name] = jnp.asarray(drawn.astype(out[name].dtype))
    for name, factor in factors.items():
        out[name] = (out[name] * factor).astype(out[name].dtype)
    return out
```

```python
from contextlib import ExitStack

import numpy as np

import concourse.bass as bass
from concourse import mybir

F32 = mybir.dt.float32
F32R = mybir.dt.float32r
BF16 = mybir.dt.bfloat16
I32 = mybir.dt.int32
U32 = mybir.dt.uint32
ALU = mybir.AluOpType
ACT = mybir.ActivationFunctionType
AX = mybir.AxisListType

IMAGES = 64
PATCHES = 14
PIX = 16
TOKENS = PATCHES * PATCHES + 1
T = 100
ROWS = 2 * T
C = 192
KIN = 3 * PIX * PIX // 128
HEADS = 12
D = C // HEADS
CH = C // 2
HID = 768
FT = HID // 128
EXPERTS = 4
SETS = 2
ALL_E = SETS * EXPERTS
NROW = IMAGES * ROWS
NTOK = IMAGES * TOKENS
CAPACITY = NTOK // EXPERTS
NT = 2 * IMAGES
EPS = 1e-5

PARTS = 3
KS = PARTS * D
MROW = KS

TS = 256
REGION = (NROW + TS - 1) // TS * TS
NULL_AT = ALL_E * REGION
LIST = NULL_AT + TS
EMPTY = 1 << 20
TILES_C = (NTOK + EXPERTS * (TS - 1)) // TS
TILES_U = (NTOK - CAPACITY + EXPERTS * (TS - 1)) // TS
TILES = TILES_C + TILES_U
BISECT = 26

W1C = 2 * HID
W2C = FT * C
SROW = C + SETS

SLOTS = 9
TAU = dict(E0=7, E1=8, STATS1=9, NORM1=10, STATS2=12, NORM2=13, N1T=16, QK0=18, QK1=19, V=20, QT0=22, QT1=23,
           S=29, MT=39, TG=43, PV=46, ONORM=54, ATT=55, PROJ=58, NORM3=60, N2T=62, LG=68)
MISC = ("N1T", "V", "MT", "ATT", "PROJ", "N2T", "LG")
LAST = max(TAU.values()) // SLOTS
UNROLL = 4
LOOP_FROM = 8
LOOP_TO = IMAGES

T_GROUPS = [("k1", 0), ("k0", 0), ("k0", 1), ("k1", 1), ("k0", 2), ("k0", 3), ("k1", 2), ("k0", 4), ("k0", 5)]
PAIR_GROUP = [T_GROUPS.index(("k0", p)) for p in range(6)]


class At:

    def __init__(self, n, u):
        self.n, self.u = n, u % UNROLL
        self.static = isinstance(n, int)

    def times(self, k, add):
        return self.n * k + add if self.static or k != 1 else self.n + add


class Step:
    def __init__(self, n, c):
        self.n, self.c = n, c
        self.static = isinstance(n, int)

    def image(self, lag):
        if self.static:
            j = self.n - lag
            return At(j, j) if 0 <= j < IMAGES else None
        return At(self.n - lag, self.c - lag)


started = []


def reg_wait(eng, sem, value, alone=False):
    if alone or eng.engine == mybir.EngineType.SP:
        value = eng.to_reg(value)
        eng.wait_ge(started[0], 1)
    eng.wait_ge(sem, value)


def wait(eng, sem, at, k, add, most=None, alone=False):
    v = at.times(k, add)
    if at.static:
        if most is not None:
            v = min(v, most)
        if v > 0:
            eng.wait_ge(sem, v)
    else:
        reg_wait(eng, sem, v, alone)


def run_steps(eng, body):
    for s in range(LOOP_FROM):
        body(Step(s, s))
    with eng.Fori(0, (LOOP_TO - LOOP_FROM) // UNROLL) as it:
        for c in range(UNROLL):
            body(Step(it * UNROLL + (LOOP_FROM + c), LOOP_FROM + c))
    for s in range(LOOP_TO, IMAGES + LAST):
        body(Step(s, s))


def misc_uses(step, slot):
    return sum(min(max(step - TAU[x] // SLOTS + (TAU[x] % SLOTS <= slot), 0), IMAGES) for x in MISC)


def misc_count(at, use):
    lag, slot = TAU[use] // SLOTS, TAU[use] % SLOTS
    if at.static:
        return 0, misc_uses(at.n + lag, slot)
    mid = IMAGES // 2
    k = len(MISC)
    return k, misc_uses(mid + lag, slot) - k * mid


def split3(eng, out, a_hi, a_lo, b_hi, b_lo, first, last):
    eng.matmul(out, a_hi, b_hi, start=first, stop=False)
    eng.matmul(out, a_hi, b_lo, start=False, stop=False)
    return eng.matmul(out, a_lo, b_hi, start=False, stop=last)


def program(nc, x, w_emb, tok_rows, pos, gamma, beta, w_qk, w_v, w_proj, w_router, b_router, cos, sin, ident, tri,
            lower, w1, w2, b1, b2, valid, out):
    ctx = ExitStack()
    with ctx:
        def sb(name, shape, dt=F32, where=ctx):
            return where.enter_context(nc.sbuf_tensor("s_" + name, shape, dt))

        def sem(name):
            return ctx.enter_context(nc.semaphore(name))

        psum = ctx.enter_context(nc.psum_tensor("psum", [128, 8, 512], F32))
        expert_in = nc.dram_tensor("expert_in", [NROW, SROW], F32, kind="Internal").ap()
        w1_parts = nc.dram_tensor("w1_parts", [ALL_E, CH, 2 * W1C], F32, kind="Internal").ap()
        w2_parts = nc.dram_tensor("w2_parts", [ALL_E, 128, 2 * W2C], F32, kind="Internal").ap()
        lists = nc.dram_tensor("lists", [LIST, 1], U32, kind="Internal").ap()
        logits = sb("logits", [T, NT, ALL_E])
        identity = sb("identity", [128, 128])
        scale_tiles = sb("scale_tiles", [T, NT, SETS])

        started[:] = [sem("started")]

        prepare(nc, sb, sem, w1, w2, w1_parts, w2_parts, identity, ident)
        attention(nc, sb, sem, psum, x, w_emb, tok_rows, pos, gamma, beta, w_qk, w_v, w_proj, w_router, b_router,
                  cos, sin, tri, identity, logits, expert_in, out)
        table = sb("table", [1, 4 * TABLE + 2], I32)
        route(nc, sb, sem, psum, logits, lower, valid, lists, expert_in, scale_tiles, table)
        experts(nc, sb, sem, psum, identity, table, lists, expert_in, w1_parts, w2_parts, b1, b2, out)


def prepare(nc, sb, sem, w1, w2, w1_parts, w2_parts, identity, ident):
    with ExitStack() as own:
        raw1 = [sb(f"raw1_{i}", [CH, W1C], F32, own) for i in range(2)]
        raw2 = [sb(f"raw2_{i}", [128, W2C], F32, own) for i in range(2)]
        part1 = [sb(f"part1_{i}", [CH, 2, W1C], F32R, own) for i in range(2)]
        part2 = [sb(f"part2_{i}", [128, 2, W2C], F32R, own) for i in range(2)]
        first = sb("first", [1, 1], F32, own)
        id_loaded = sem("id_loaded")
        raw_loaded = [sem(f"raw_loaded{i}") for i in range(2)]
        hi_done, lo1_done, lo2_done = sem("whi_done"), sem("wlo1_done"), sem("wlo2_done")
        stored = [sem(f"w_stored{i}") for i in range(2)]
        with nc.Block() as block:
            def store(sp, e):
                sp.wait_ge(lo1_done, e + 1)
                sp.wait_ge(lo2_done, e + 1)
                sp.dma_start(w1_parts[e], part1[e % 2][:].bitcast(F32).rearrange("p a n -> p (a n)"))\
                    .then_inc(stored[e % 2], 16)
                sp.dma_start(w2_parts[e], part2[e % 2][:].bitcast(F32).rearrange("p a n -> p (a n)"))\
                    .then_inc(stored[e % 2], 16)

            @block.sync
            def _(sp):
                sp.dma_start(identity[:], ident).then_inc(id_loaded, 16)
                for e in range(ALL_E):
                    if e >= 2:
                        sp.wait_ge(lo1_done, e - 1)
                        sp.wait_ge(lo2_done, e - 1)
                    sp.dma_start(raw1[e % 2][:], w1[e]).then_inc(raw_loaded[e % 2], 16)
                    sp.dma_start(raw2[e % 2][:], w2[e]).then_inc(raw_loaded[e % 2], 16)
                    if e >= 1:
                        store(sp, e - 1)
                store(sp, ALL_E - 1)
                sp.wait_ge(id_loaded, 16)
                for i in range(2):
                    sp.wait_ge(stored[i], 32 * (ALL_E // 2))

            @block.gpsimd
            def _(pool):
                pool.memset(first[:], 0.0).then_inc(started[0], 1)

            @block.scalar
            def _(act):
                for e in range(ALL_E):
                    act.wait_ge(raw_loaded[e % 2], 32 * (e // 2 + 1))
                    if e >= 2:
                        act.wait_ge(stored[e % 2], 32 * (e // 2))
                    act.copy(part1[e % 2][:, 0, :], raw1[e % 2][:])
                    act.copy(part2[e % 2][:, 0, :], raw2[e % 2][:]).then_inc(hi_done, 1)

            @block.vector
            def _(dve):
                for e in range(ALL_E):
                    dve.wait_ge(hi_done, e + 1)
                    dve.tensor_tensor(part1[e % 2][:, 1, :], raw1[e % 2][:], part1[e % 2][:, 0, :].bitcast(F32),
                                      ALU.subtract).then_inc(lo1_done, 1)
                    dve.tensor_tensor(part2[e % 2][:, 1, :], raw2[e % 2][:], part2[e % 2][:, 0, :].bitcast(F32),
                                      ALU.subtract).then_inc(lo2_done, 1)


def attention(nc, sb, sem, psum, x, w_emb, tok_rows, pos, gamma, beta, w_qk, w_v, w_proj, w_router, b_router,
              cos, sin, tri, identity, logits, expert_in, out):
    with ExitStack() as own:
        def buf(name, shape, dt=F32):
            return sb(name, shape, dt, own)

        wemb = buf("wemb", [128, KIN, C])
        table = buf("tok_table", [T, 2, C])
        pos_sb = buf("pos", [T, 2, C])
        gamma_sb = buf("gamma", [T, C])
        beta_sb = buf("beta", [T, C])
        br_sb = buf("b_router", [T, ALL_E])
        cos_sb = buf("cos", [T, 2, D])
        sin_sb = buf("sin", [T, 2, D])
        tri_raw = buf("tri_raw", [T, 4, T])
        tri_sb = buf("tri_sb", [T, 4, T], BF16)
        eye16 = buf("eye16", [T, T], BF16)
        half = buf("minus_half", [T, 2])
        raw = buf("raw_w", [CH, 2, 3 * C + C + ALL_E])
        whi = buf("w_hi", [CH, 2, 3 * C + C + ALL_E], F32R)
        wlo = buf("w_lo", [CH, 2, 3 * C + C + ALL_E], F32R)
        QK, VV, PJ, RT = (slice(0, 2 * C), slice(2 * C, 3 * C), slice(3 * C, 4 * C), slice(4 * C, 4 * C + ALL_E))

        x_in = [buf(f"x_in{i}", [128, KIN, ROWS]) for i in range(2)]
        xs = buf("xs", [T, 2, C])
        xn = buf("xn", [T, 2, C])
        h_new = [buf(f"h_new{i}", [T, 2, C]) for i in range(2)]
        h_old = [buf(f"h_old{i}", [T, 2, C]) for i in range(2)]
        stat = [buf(f"stat{i}", [T, 2, 6]) for i in range(3)]
        mv = [buf(f"mv{i}", [T, 2, 2]) for i in range(3)]
        var_eps = [buf(f"var_eps{i}", [T, 2]) for i in range(3)]
        rstd = [buf(f"rstd{i}", [T, 2]) for i in range(3)]
        n1 = buf("n1", [T, 2, C])
        n1t = [buf("n1t_hi", [CH, 2, ROWS], F32R), buf("n1t_lo", [CH, 2, ROWS], F32R)]
        roped = [buf(f"rope_cos{i}", [T, 2 * C]) for i in range(2)]
        ropes = [buf(f"rope_sin{i}", [T, 2 * C]) for i in range(2)]
        qkr = buf("qk_rot", [T, 2, 2 * C])
        v_aug = [buf(f"v_aug{i}", [T, 2, HEADS, D + 1]) for i in range(4)]
        qkt = [buf("qkt_hi", [CH, 4, ROWS], F32R), buf("qkt_lo", [CH, 4, ROWS], F32R)]
        q_st = [buf(f"q_stack{i}", [KS + 1, HEADS, ROWS], F32R) for i in range(4)]
        k_st = [buf(f"k_stack{i}", [KS + 1, HEADS, ROWS], F32R) for i in range(4)]
        rmax = [buf(f"row_max{i}", [T, 2, HEADS]) for i in range(2)]
        rmax_t = buf("row_max_t", [HEADS, ROWS], F32R)
        p0 = [buf(f"p_k0_{i}", [T, HEADS, ROWS]) for i in range(2)]
        p1 = [buf(f"p_k1_{i}", [T, HEADS, T]) for i in range(2)]
        rden = buf("rden", [T, 2, HEADS])
        att = buf("att", [T, 2, C])
        att_t = [buf("att_t_hi", [CH, 2, ROWS], F32R), buf("att_t_lo", [CH, 2, ROWS], F32R)]
        h1 = [buf(f"h1_{i}", [T, 2, C]) for i in range(2)]
        n2 = [buf(f"n2_{i}", [T, 2, C]) for i in range(2)]
        n2t = [buf("n2t_hi", [CH, 2, ROWS], F32R), buf("n2t_lo", [CH, 2, ROWS], F32R)]

        h_dram = nc.dram_tensor("h_dram", [IMAGES, T, 2, C], F32, kind="Internal").ap()
        qk_dram = [[nc.dram_tensor(f"qk_dram{i}_{a}", [2 * C, ROWS], F32, kind="Internal").ap() for a in range(2)]
                   for i in range(2)]
        max_dram = [nc.dram_tensor(f"max_dram{i}", [HEADS, ROWS], F32, kind="Internal").ap() for i in range(2)]

        s_bank = [psum[:, 0, :], psum[:, 1, :]]
        t_bank = [psum[:, 2, :], psum[:, 3, :]]
        q_bank = [psum[:, 4, :], psum[:, 5, :]]
        o_bank = psum[:, 6, :]
        m_bank = psum[:, 7, :]
        m_half = m_bank[0:CH, 0:2 * ROWS]
        m_rows = m_bank[0:T, 0:2 * C].rearrange("p (t c) -> p t c", t=2)

        const_loaded, const_ready, w_ready = sem("const_loaded"), sem("const_ready"), sem("w_ready")
        ms = sem("set_once")
        x_loaded = [sem(f"x_loaded{i}") for i in range(2)]
        emb_done = [sem("emb_done0"), sem("emb_done1")]
        emb_sum = [sem("emb_sum0"), sem("emb_sum1")]
        bn = [sem(f"bn_done{i}") for i in range(3)]
        mv_done = [sem(f"mv_done{i}") for i in range(3)]
        ve_done = [sem(f"ve_done{i}") for i in range(3)]
        rs_done = [sem(f"rs_done{i}") for i in range(3)]
        norm1, gamma_done, h_done = sem("norm1"), sem("gamma_done"), sem("h_done")
        h_stored = [sem(f"h_stored{i}") for i in range(2)]
        h_loaded = [sem(f"h_loaded{i}") for i in range(2)]
        n1_done, n1t_done, n1hi_done = sem("n1_done"), sem("n1t_done"), sem("n1hi_done")
        qk_done = [sem("qk_done0"), sem("qk_done1")]
        v_done = sem("v_done")
        rope_mul = [sem("rope_mul0"), sem("rope_mul1")]
        rope_add = [sem("rope_add0"), sem("rope_add1")]
        qt_done = [sem("qt_done0"), sem("qt_done1")]
        qhi_done = [sem("qhi_done0"), sem("qhi_done1")]
        qlo_done = [sem("qlo_done0"), sem("qlo_done1")]
        qk_stored = [sem(f"qk_stored{i}") for i in range(2)]
        stacked = [sem(f"stacked{i}") for i in range(4)]
        s_done, max_done = sem("s_done"), sem("max_done")
        mt_done, max_stored, max_placed = sem("mt_done"), sem("max_stored"), sem("max_placed")
        t_done, exp_done, masked = sem("t_done"), sem("exp_done"), sem("masked")
        pv_done, rden_done, onorm = sem("pv_done"), sem("rden_done"), sem("onorm")
        att_tr, att_hi, proj_done, h1_done_ = sem("att_tr"), sem("att_hi"), sem("proj_done"), sem("h1_done_")
        n2_done, n2t_done, n2hi_done, lg_done = sem("n2_done"), sem("n2t_done"), sem("n2hi_done"), sem("lg_done")
        rows_stored = [sem(f"rows_stored{i}") for i in range(2)]
        misc_read = sem("misc_read")

        def misc_free(pe, at, use):
            k, add = misc_count(at, use)
            wait(pe, misc_read, at, k, add - 1)

        def misc_over(eng, at, use):
            k, add = misc_count(at, use)
            wait(eng, misc_read, at, k, add)

        def wait_dma(eng, sems, at, per, back=0):
            n = len(sems)
            if at.static:
                j = at.n - back
                if j >= 0:
                    eng.wait_ge(sems[j % n], per * (j // n + 1))
                return
            u = (at.u - back) % n
            assert per % n == 0
            reg_wait(eng, sems[u], (at.n - back) * (per // n) + (per - per // n * u))

        with nc.Block() as block:
            @block.sync
            def _(sp):
                sp.dma_start(wemb[:], w_emb).then_inc(const_loaded, 16)
                sp.dma_start(table[:], tok_rows).then_inc(const_loaded, 16)
                sp.dma_start(pos_sb[:], pos).then_inc(const_loaded, 16)
                sp.dma_start(gamma_sb[:], gamma.partition_broadcast(T)).then_inc(const_loaded, 16)
                sp.dma_start(beta_sb[:], beta.partition_broadcast(T)).then_inc(const_loaded, 16)
                sp.dma_start(br_sb[:], b_router.partition_broadcast(T)).then_inc(const_loaded, 16)
                sp.dma_start(cos_sb[:], cos).then_inc(const_loaded, 16)
                sp.dma_start(sin_sb[:], sin).then_inc(const_loaded, 16)
                sp.dma_start(tri_raw[:], tri).then_inc(const_loaded, 16)
                sp.dma_start(raw[:, :, QK], w_qk).then_inc(const_loaded, 16)
                sp.dma_start(raw[:, :, VV], w_v).then_inc(const_loaded, 16)
                sp.dma_start(raw[:, :, PJ], w_proj).then_inc(const_loaded, 16)
                sp.dma_start(raw[:, :, RT], w_router).then_inc(const_loaded, 16)

                sp.wait_ge(ms, 9)

                def load_x(at):
                    if at is None:
                        return
                    wait(sp, emb_done[1], at, 1, -1)
                    sp.dma_start(x_in[at.u % 2][:], x[bass.ds(at.n, 1)].rearrange("b p k t -> (b p) k t"))\
                        .then_inc(x_loaded[at.u % 2], 16)

                def store_h(at):
                    if at is None:
                        return
                    wait(sp, h_done, at, 1, 1)
                    sp.dma_start(h_dram[bass.ds(at.n, 1)].rearrange("b p t c -> (b p) t c"), h_new[at.u % 2][:])\
                        .then_inc(h_stored[at.u % 2], 16)

                def load_h(at):
                    if at is None:
                        return
                    wait_dma(sp, h_stored, at, 16)
                    misc_over_back(sp, at, "PROJ", 2)
                    sp.dma_start(h_old[at.u % 2][:], h_dram[bass.ds(at.n, 1)].rearrange("b p t c -> (b p) t c"))\
                        .then_inc(h_loaded[at.u % 2], 16)

                def place_max(at):
                    if at is None:
                        return
                    misc_over(sp, at, "MT")
                    wait(sp, max_placed, at, 16, 0)
                    sp.dma_start(max_dram[at.u % 2], rmax_t[:].bitcast(F32)).then_inc(max_stored, 16)
                    wait(sp, max_stored, at, 16, 16)
                    sp.dma_start(q_st[at.u][MROW:MROW + 1].bitcast(F32), max_dram[at.u % 2].unsqueeze(0))\
                        .then_inc(max_placed, 16)

                def stack(at):
                    if at is None:
                        return
                    for a, done in enumerate((qhi_done, qlo_done)):
                        wait(sp, done[0], at, 1, 1)
                        wait(sp, done[1], at, 1, 1)
                        wait_dma(sp, stacked, at, 96, back=2)
                        sp.dma_start(qk_dram[at.u % 2][a].rearrange("(c p) t -> p c t", p=CH), qkt[a][:].bitcast(F32))\
                            .then_inc(qk_stored[at.u % 2], 16)
                    wait(sp, t_done, at, SLOTS, -3 * SLOTS)
                    wait_dma(sp, qk_stored, at, 32)
                    for r, (qa, ka) in enumerate(((0, 0), (1, 0), (0, 1))):
                        for st, a, c in ((q_st, qa, 0), (k_st, ka, 1)):
                            sp.dma_start(st[at.u][r * D:(r + 1) * D].bitcast(F32),
                                         qk_dram[at.u % 2][a][c * C:(c + 1) * C].rearrange("(h d) t -> d h t", d=D))\
                                .then_inc(stacked[at.u], 16)

                def store_rows(at):
                    if at is None:
                        return
                    wait(sp, n2_done, at, 1, 1)
                    rows = expert_in.rearrange("(b t p) c -> b p t c", b=IMAGES, t=2)
                    sp.dma_start(rows[bass.ds(at.n, 1), :, :, 0:C].rearrange("b p t c -> (b p) t c"), n2[at.u % 2][:])\
                        .then_inc(rows_stored[at.u % 2], 16)
                    rows = out.rearrange("(b t p) c -> b p t c", b=IMAGES, t=2)
                    sp.dma_start(rows[bass.ds(at.n, 1)].rearrange("b p t c -> (b p) t c"), h1[at.u % 2][:])\
                        .then_inc(rows_stored[at.u % 2], 16)

                def misc_over_back(eng, at, use, back):
                    if at.static:
                        if at.n >= back:
                            misc_over(eng, At(at.n - back, 0), use)
                    else:
                        misc_over(eng, At(at.n - back, 0), use)

                def step(s):
                    load_x(s.image(0))
                    place_max(s.image(4))
                    store_h(s.image(1))
                    load_h(s.image(5))
                    stack(s.image(2))
                    store_rows(s.image(6))
                run_steps(sp, step)
                for i in range(2):
                    sp.wait_ge(rows_stored[i], 32 * IMAGES // 2)

            @block.tensor
            def _(pe):
                pe.wait_ge(w_ready, 4)
                pe.wait_ge(const_ready, 3)
                pe.wait_ge(ms, 9)

                def embed(at, t):
                    if at is None:
                        return
                    if t == 0:
                        wait_dma(pe, x_loaded, at, 16)
                    wait(pe, qlo_done[t], at, 1, -1)
                    for k in range(KIN):
                        mm = pe.matmul(q_bank[t][0:T, 0:C], x_in[at.u % 2][:, k, t * T:(t + 1) * T], wemb[:, k, :],
                                       start=(k == 0), stop=(k == KIN - 1))
                    mm.then_inc(emb_done[t], 1)

                def turn(src, done):
                    for t in range(2):
                        for c in range(2):
                            mm = pe.transpose(m_half[:, c * ROWS + t * T:c * ROWS + (t + 1) * T],
                                              src[:, t, c * CH:(c + 1) * CH], identity[0:T, 0:T])
                    mm.then_inc(done, 1)

                def n1_turn(at):
                    if at is None:
                        return
                    misc_free(pe, at, "N1T")
                    wait(pe, n1_done, at, 1, 1)
                    turn(n1, n1t_done)

                def qk(at, t):
                    if at is None:
                        return
                    if t == 0:
                        misc_over(pe, at, "N1T")
                    wait(pe, emb_sum[t], at, 1, 2, IMAGES)
                    for c in range(2):
                        mm = split3(pe, q_bank[t][0:T, 0:2 * C], n1t[0][:, c, t * T:(t + 1) * T],
                                    n1t[1][:, c, t * T:(t + 1) * T], whi[:, c, QK], wlo[:, c, QK], c == 0, c == 1)
                    mm.then_inc(qk_done[t], 1)

                def v(at):
                    if at is None:
                        return
                    misc_free(pe, at, "V")
                    for t in range(2):
                        for c in range(2):
                            mm = split3(pe, m_rows[:, t, :], n1t[0][:, c, t * T:(t + 1) * T],
                                        n1t[1][:, c, t * T:(t + 1) * T], whi[:, c, VV], wlo[:, c, VV], c == 0, c == 1)
                    mm.then_inc(v_done, 1)

                def qk_turn(at, b):
                    if at is None:
                        return
                    wait(pe, rope_mul[b], at, 1, 1)
                    for t in range(2):
                        wait(pe, rope_add[t], at, 1, 1)
                    for cc in range(2):
                        for t in range(2):
                            col = (2 * b + cc) * CH
                            mm = pe.transpose(q_bank[b][0:CH, cc * ROWS + t * T:cc * ROWS + (t + 1) * T],
                                              qkr[:, t, col:col + CH], identity[0:T, 0:T])
                    mm.then_inc(qt_done[b], 1)

                def scores(at, g):
                    if at is None:
                        return
                    if g == 0:
                        wait_dma(pe, stacked, at, 96)
                    wait(pe, max_done, at, SLOTS, g - 1)
                    bank = s_bank[(at.u + g) % 2]
                    q, k = q_st[at.u], k_st[at.u]
                    if g < 3:
                        pe.matmul(bank[0:T, 0:4 * T], eye16[:], tri_sb[:].rearrange("p a b -> p (a b)"),
                                  start=True, stop=False, skip_group_check=True)
                        for i in range(4):
                            h = 4 * g + i
                            mm = pe.matmul(bank[0:T, i * T:(i + 1) * T], q[0:KS, h, 0:T], k[0:KS, h, 0:T],
                                           start=False, stop=(i == 3), skip_group_check=True)
                    else:
                        two_heads = bank[0:T, 0:2 * ROWS].rearrange("p (h k) -> p h k", h=2)
                        pe.matmul(two_heads[:, :, T:ROWS], eye16[:], tri_sb[:, 0:2, :],
                                  start=True, stop=False, skip_group_check=True)
                        for i in range(2):
                            h = 2 * (g - 3) + i
                            mm = pe.matmul(two_heads[:, i, :], q[0:KS, h, T:ROWS], k[0:KS, h, :],
                                           start=False, stop=(i == 1), skip_group_check=True)
                    mm.then_inc(s_done, 1)

                def max_turn(at):
                    if at is None:
                        return
                    misc_free(pe, at, "MT")
                    wait(pe, max_done, at, SLOTS, SLOTS)
                    for t in range(2):
                        mm = pe.transpose(m_bank[0:HEADS, t * T:(t + 1) * T], rmax[at.u % 2][:, t, :], identity[0:T, 0:T])
                    mm.then_inc(mt_done, 1)

                def scores_t(at, g):
                    if at is None:
                        return
                    if g == 0:
                        wait(pe, max_placed, at, 16, 16)
                    wait(pe, exp_done, at, SLOTS, g - 1)
                    bank = t_bank[(at.u + g) % 2]
                    q, k = q_st[at.u], k_st[at.u]
                    kind, n = T_GROUPS[g]
                    if kind == "k1":
                        for i in range(4):
                            mm = pe.matmul(bank[0:T, i * T:(i + 1) * T], k[:, 4 * n + i, T:ROWS], q[:, 4 * n + i, T:ROWS],
                                           start=True, stop=True)
                    else:
                        for i in range(2):
                            mm = pe.matmul(bank[0:T, i * ROWS:(i + 1) * ROWS], k[:, 2 * n + i, 0:T], q[:, 2 * n + i, :],
                                           start=True, stop=True)
                    mm.then_inc(t_done, 1)

                def pv(at, pair):
                    if at is None:
                        return
                    if pair == 0:
                        wait(pe, onorm, at, 1, 0)
                        misc_over(pe, at, "V")
                    wait(pe, masked, at, SLOTS, PAIR_GROUP[pair] + 1)
                    for h in (2 * pair, 2 * pair + 1):
                        o = [o_bank[0:T, (t * HEADS + h) * (D + 1):(t * HEADS + h + 1) * (D + 1)] for t in range(2)]
                        pr, va = p0[at.u % 2], v_aug[at.u]
                        pe.matmul(o[0], pr[:, h, 0:T], va[:, 0, h, :], start=True, stop=True)
                        pe.matmul(o[1], pr[:, h, T:ROWS], va[:, 0, h, :], start=True, stop=False)
                        mm = pe.matmul(o[1], p1[at.u % 2][:, h, :], va[:, 1, h, :], start=False, stop=True)
                    mm.then_inc(pv_done, 1)

                def att_turn(at):
                    if at is None:
                        return
                    misc_free(pe, at, "ATT")
                    wait(pe, onorm, at, 1, 1)
                    turn(att, att_tr)

                def project(at):
                    if at is None:
                        return
                    misc_free(pe, at, "PROJ")
                    for t in range(2):
                        for c in range(2):
                            mm = split3(pe, m_rows[:, t, :], att_t[0][:, c, t * T:(t + 1) * T],
                                        att_t[1][:, c, t * T:(t + 1) * T], whi[:, c, PJ], wlo[:, c, PJ], c == 0, c == 1)
                    mm.then_inc(proj_done, 1)

                def n2_turn(at):
                    if at is None:
                        return
                    misc_free(pe, at, "N2T")
                    wait(pe, n2_done, at, 1, 1)
                    turn(n2[at.u % 2], n2t_done)

                def router(at):
                    if at is None:
                        return
                    misc_free(pe, at, "LG")
                    for t in range(2):
                        for c in range(2):
                            mm = split3(pe, m_bank[0:T, t * ALL_E:(t + 1) * ALL_E], n2t[0][:, c, t * T:(t + 1) * T],
                                        n2t[1][:, c, t * T:(t + 1) * T], whi[:, c, RT], wlo[:, c, RT], c == 0, c == 1)
                    mm.then_inc(lg_done, 1)

                def step(s):
                    i = s.image
                    scores(i(4), 7)
                    scores_t(i(5), 2)
                    qk(i(2), 0)
                    scores(i(4), 8)
                    scores_t(i(5), 3)
                    pv(i(5), 0)
                    att_turn(i(6))
                    qk(i(2), 1)
                    scores(i(3), 0)
                    scores_t(i(5), 4)
                    pv(i(5), 1)
                    v(i(2))
                    scores(i(3), 1)
                    scores_t(i(5), 5)
                    max_turn(i(4))
                    scores(i(3), 2)
                    scores_t(i(5), 6)
                    pv(i(5), 2)
                    project(i(6))
                    qk_turn(i(2), 0)
                    scores(i(3), 3)
                    scores_t(i(5), 7)
                    pv(i(5), 3)
                    router(i(7))
                    qk_turn(i(2), 1)
                    scores(i(3), 4)
                    scores_t(i(5), 8)
                    scores(i(3), 5)
                    scores_t(i(4), 0)
                    pv(i(5), 4)
                    n1_turn(i(1))
                    embed(i(0), 0)
                    scores(i(3), 6)
                    scores_t(i(4), 1)
                    pv(i(5), 5)
                    n2_turn(i(6))
                    embed(i(0), 1)
                run_steps(pe, step)

            @block.scalar
            def _(act):
                act.wait_ge(const_loaded, 16 * 13)
                act.wait_ge(ms, 9)
                for c in range(2):
                    act.copy(whi[:, c, :], raw[:, c, :]).then_inc(w_ready, 1)

                def n1_hi(at):
                    if at is None:
                        return
                    wait(act, n1t_done, at, 1, 1)
                    wait(act, v_done, at, 1, 0)
                    act.copy(n1t[0][:].rearrange("p a b -> p (a b)"), m_half).then_inc(n1hi_done, 1)

                def values(at):
                    if at is None:
                        return
                    wait(act, v_done, at, 1, 1)
                    wait(act, pv_done, at, 6, -18)
                    act.copy(v_aug[at.u][:, :, :, 0:D], m_rows.rearrange("p t (h d) -> p t h d", d=D))\
                        .then_inc(misc_read, 1)

                def qk_hi(at, b):
                    if at is None:
                        return
                    wait(act, qt_done[b], at, 1, 1)
                    wait_dma(act, qk_stored, at, 32, back=1)
                    act.copy(qkt[0][:, 2 * b:2 * b + 2, :].rearrange("p a b -> p (a b)"), q_bank[b][0:CH, 0:2 * ROWS])\
                        .then_inc(qhi_done[b], 1)

                def max_out(at):
                    if at is None:
                        return
                    wait(act, mt_done, at, 1, 1)
                    wait(act, max_stored, at, 16, 0)
                    act.copy(rmax_t[:], m_bank[0:HEADS, 0:ROWS]).then_inc(misc_read, 1)

                def exps(at, g):
                    if at is None:
                        return
                    wait(act, t_done, at, SLOTS, g + 1)
                    wait(act, pv_done, at, 6, -6)
                    kind, n = T_GROUPS[g]
                    bank = t_bank[(at.u + g) % 2][0:T, 0:2 * ROWS]
                    dst = p1[at.u % 2][:, 4 * n:4 * n + 4, :] if kind == "k1" else p0[at.u % 2][:, 2 * n:2 * n + 2, :]
                    act.activation(dst.rearrange("p a b -> p (a b)"), bank, ACT.Exp, scale=float(D) ** -0.5)\
                        .then_inc(exp_done, 1)

                def att_hi_part(at):
                    if at is None:
                        return
                    wait(act, att_tr, at, 1, 1)
                    wait(act, proj_done, at, 1, 0)
                    act.copy(att_t[0][:].rearrange("p a b -> p (a b)"), m_half).then_inc(att_hi, 1)

                def n2_hi(at):
                    if at is None:
                        return
                    wait(act, n2t_done, at, 1, 1)
                    wait(act, lg_done, at, 1, 0)
                    act.copy(n2t[0][:].rearrange("p a b -> p (a b)"), m_half).then_inc(n2hi_done, 1)

                def step(s):
                    i = s.image
                    exps(i(5), 2)
                    exps(i(5), 3)
                    att_hi_part(i(6))
                    exps(i(5), 4)
                    values(i(2))
                    exps(i(5), 5)
                    max_out(i(4))
                    exps(i(5), 6)
                    qk_hi(i(2), 0)
                    exps(i(5), 7)
                    qk_hi(i(2), 1)
                    exps(i(5), 8)
                    exps(i(4), 0)
                    n1_hi(i(1))
                    exps(i(4), 1)
                    n2_hi(i(6))
                run_steps(act, step)

            @block.vector
            def _(dve):
                dve.wait_ge(const_loaded, 16 * 13)
                dve.tensor_tensor(table[:], table[:], pos_sb[:], ALU.add).then_inc(const_ready, 1)
                dve.tensor_copy(eye16[:], identity[0:T, 0:T]).then_inc(const_ready, 1)
                dve.tensor_copy(tri_sb[:], tri_raw[:]).then_inc(const_ready, 1)
                dve.wait_ge(w_ready, 2)
                for c in range(2):
                    dve.tensor_tensor(wlo[:, c, :], raw[:, c, :], whi[:, c, :].bitcast(F32), ALU.subtract)\
                        .then_inc(w_ready, 1)
                dve.wait_ge(const_ready, 3)

                def sum_rows(at, t):
                    if at is None:
                        return
                    wait(dve, emb_done[t], at, 1, 1)
                    dve.tensor_tensor(xs[:, t, :], q_bank[t][0:T, 0:C], table[:, t, :], ALU.add).then_inc(emb_sum[t], 1)

                def stats(at, n, src):
                    for t in range(2):
                        ins = dve.bn_stats(stat[n][:, t, :], src[:, t, :])
                    ins.then_inc(bn[n], 1)
                    wait(dve, bn[n], at, 1, 1, alone=True)
                    for t in range(2):
                        ins = dve.bn_aggr(mv[n][:, t, :], stat[n][:, t, :])
                    ins.then_inc(mv_done[n], 1)

                def norm(at, n, src, dst, done):
                    wait(dve, rs_done[n], at, 1, 1)
                    for t in range(2):
                        ins = dve.tensor_scalar(dst[:, t, :], src[:, t, :], mv[n][:, t, 0:1], rstd[n][:, t:t + 1],
                                                ALU.subtract, ALU.mult)
                    ins.then_inc(done, 1)

                def stats1(at):
                    if at is None:
                        return
                    wait(dve, emb_sum[1], at, 1, 1)
                    stats(at, 0, xs)

                def norm1_rows(at):
                    if at is None:
                        return
                    wait(dve, h_done, at, 1, 0)
                    norm(at, 0, xs, xn, norm1)

                def stats2(at):
                    if at is None:
                        return
                    wait(dve, h_done, at, 1, 1)
                    stats(at, 1, h_new[at.u % 2])

                def norm2_rows(at):
                    if at is None:
                        return
                    wait(dve, n1t_done, at, 1, 0)
                    norm(at, 1, h_new[at.u % 2], n1, n1_done)

                def n1_lo(at):
                    if at is None:
                        return
                    wait(dve, n1hi_done, at, 1, 1)
                    dve.tensor_tensor(n1t[1][:].rearrange("p a b -> p (a b)"), m_half,
                                      n1t[0][:].bitcast(F32).rearrange("p a b -> p (a b)"), ALU.subtract)\
                        .then_inc(misc_read, 1)

                def rope(at, t):
                    if at is None:
                        return
                    wait(dve, qk_done[t], at, 1, 1)
                    wait(dve, rope_add[t], at, 1, 0)
                    heads = 2 * HEADS
                    src = q_bank[t][0:T, 0:2 * C].rearrange("p (h d) -> p h d", d=D)
                    dc = roped[t][:].rearrange("p (h d) -> p h d", d=D)
                    ds = ropes[t][:].rearrange("p (h d) -> p h d", d=D)
                    cosb = cos_sb[:, t, :].unsqueeze(1).to_broadcast([T, heads, D])
                    dve.tensor_tensor(dc, src, cosb, ALU.mult)
                    for a in range(2):
                        to, fr = slice(a * D // 2, (a + 1) * D // 2), slice((1 - a) * D // 2, (2 - a) * D // 2)
                        ins = dve.tensor_tensor(ds[:, :, to], src[:, :, fr],
                                                sin_sb[:, t, to].unsqueeze(1).to_broadcast([T, heads, D // 2]), ALU.mult)
                    ins.then_inc(rope_mul[t], 1)

                def qk_lo(at, b):
                    if at is None:
                        return
                    wait(dve, qhi_done[b], at, 1, 1)
                    wait_dma(dve, qk_stored, at, 32, back=1)
                    dve.tensor_tensor(qkt[1][:, 2 * b:2 * b + 2, :].rearrange("p a b -> p (a b)"),
                                      q_bank[b][0:CH, 0:2 * ROWS],
                                      qkt[0][:, 2 * b:2 * b + 2, :].bitcast(F32).rearrange("p a b -> p (a b)"),
                                      ALU.subtract).then_inc(qlo_done[b], 1)

                def row_max(at, g):
                    if at is None:
                        return
                    wait(dve, s_done, at, SLOTS, g + 1)
                    if g == 0:
                        wait(dve, mt_done, at, 1, -1)
                    bank = s_bank[(at.u + g) % 2][0:T, 0:2 * ROWS]
                    if g < 3:
                        dve.tensor_reduce(rmax[at.u % 2][:, 0, 4 * g:4 * g + 4], bank.rearrange("p (h k) -> p h k", h=4),
                                          AX.X, ALU.max).then_inc(max_done, 1)
                    else:
                        dve.tensor_reduce(rmax[at.u % 2][:, 1, 2 * (g - 3):2 * (g - 3) + 2],
                                          bank.rearrange("p (h k) -> p h k", h=2), AX.X, ALU.max).then_inc(max_done, 1)

                def normalise(at):
                    if at is None:
                        return
                    wait(dve, pv_done, at, 6, 6)
                    o = o_bank[0:T, 0:2 * HEADS * (D + 1)].rearrange("p (h d) -> p h d", d=D + 1)
                    dve.reciprocal(rden[:].rearrange("p t h -> p (t h)"), o[:, :, D]).then_inc(rden_done, 1)
                    wait(dve, rden_done, at, 1, 1)
                    wait(dve, att_tr, at, 1, 0)
                    dve.tensor_tensor(att[:].rearrange("p t (h d) -> p (t h) d", d=D), o[:, :, 0:D],
                                      rden[:].rearrange("p t h -> p (t h)").unsqueeze(2)
                                      .to_broadcast([T, 2 * HEADS, D]), ALU.mult).then_inc(onorm, 1)

                def att_lo(at):
                    if at is None:
                        return
                    wait(dve, att_hi, at, 1, 1)
                    dve.tensor_tensor(att_t[1][:].rearrange("p a b -> p (a b)"), m_half,
                                      att_t[0][:].bitcast(F32).rearrange("p a b -> p (a b)"), ALU.subtract)\
                        .then_inc(misc_read, 1)

                def residual(at):
                    if at is None:
                        return
                    wait(dve, proj_done, at, 1, 1)
                    wait_dma(dve, h_loaded, at, 16)
                    wait_dma(dve, rows_stored, at, 32, back=2)
                    dve.tensor_tensor(h1[at.u % 2][:], m_rows, h_old[at.u % 2][:], ALU.add).then_inc(misc_read, 1)
                    misc_over(dve, at, "PROJ")
                    stats(at, 2, h1[at.u % 2])

                def norm3_rows(at):
                    if at is None:
                        return
                    wait(dve, n2t_done, at, 1, -1)
                    norm(at, 2, h1[at.u % 2], n2[at.u % 2], n2_done)

                def n2_lo(at):
                    if at is None:
                        return
                    wait(dve, n2hi_done, at, 1, 1)
                    dve.tensor_tensor(n2t[1][:].rearrange("p a b -> p (a b)"), m_half,
                                      n2t[0][:].bitcast(F32).rearrange("p a b -> p (a b)"), ALU.subtract)\
                        .then_inc(misc_read, 1)

                def add_router_bias(at):
                    if at is None:
                        return
                    wait(dve, lg_done, at, 1, 1)
                    dve.tensor_tensor(logits[:, bass.ds(at.n * 2, 2), :],
                                      m_bank[0:T, 0:2 * ALL_E].rearrange("p (t e) -> p t e", t=2),
                                      br_sb[:].unsqueeze(1).to_broadcast([T, 2, ALL_E]), ALU.add).then_inc(misc_read, 1)

                def step(s):
                    i = s.image
                    sum_rows(s.image(1), 1)
                    row_max(i(4), 7)
                    normalise(i(6))
                    rope(i(2), 0)
                    stats1(i(1))
                    row_max(i(4), 8)
                    norm1_rows(i(1))
                    att_lo(i(6))
                    rope(i(2), 1)
                    row_max(i(3), 0)
                    row_max(i(3), 1)
                    stats2(i(1))
                    row_max(i(3), 2)
                    norm2_rows(i(1))
                    residual(i(6))
                    qk_lo(i(2), 0)
                    row_max(i(3), 3)
                    add_router_bias(i(7))
                    qk_lo(i(2), 1)
                    row_max(i(3), 4)
                    norm3_rows(i(6))
                    row_max(i(3), 5)
                    n1_lo(i(1))
                    row_max(i(3), 6)
                    n2_lo(i(6))
                    sum_rows(i(0), 0)
                run_steps(dve, step)

            @block.gpsimd
            def _(pool):
                for i in range(4):
                    if i >= 1:
                        pool.wait_ge(ms, 2 * i)
                    pool.memset(v_aug[i][:], 1.0).then_inc(ms, 1)
                    pool.wait_ge(ms, 2 * i + 1)
                    pool.memset(k_st[i][KS - D:KS + 1].bitcast(F32), -1.0).then_inc(ms, 1)
                pool.wait_ge(ms, 8)
                pool.memset(half[:], -0.5).then_inc(ms, 1)
                pool.wait_ge(ms, 9)

                def root(at, n):
                    wait(pool, mv_done[n], at, 1, 1, alone=True)
                    pool.tensor_scalar(var_eps[n][:], mv[n][:, :, 1], EPS, None, ALU.add).then_inc(ve_done[n], 1)
                    wait(pool, ve_done[n], at, 1, 1)
                    pool.tensor_tensor(rstd[n][:], var_eps[n][:], half[:], ALU.pow).then_inc(rs_done[n], 1)

                def root_of(at, n):
                    if at is not None:
                        root(at, n)

                def affine(at):
                    if at is None:
                        return
                    wait(pool, norm1, at, 1, 1)
                    g = gamma_sb[:].unsqueeze(1).to_broadcast([T, 2, C])
                    b = beta_sb[:].unsqueeze(1).to_broadcast([T, 2, C])
                    pool.tensor_tensor(xn[:], xn[:], g, ALU.mult).then_inc(gamma_done, 1)
                    wait(pool, gamma_done, at, 1, 1)
                    wait(pool, n1_done, at, 1, -1)
                    wait_dma(pool, h_stored, at, 16, back=2)
                    pool.tensor_tensor(h_new[at.u % 2][:], xn[:], b, ALU.add).then_inc(h_done, 1)

                def rope_sum(at, t):
                    if at is None:
                        return
                    wait(pool, rope_mul[t], at, 1, 1)
                    wait(pool, qt_done[1], at, 1, 0)
                    pool.tensor_tensor(qkr[:, t, :], roped[t][:], ropes[t][:], ALU.add).then_inc(rope_add[t], 1)

                def causal(at, g):
                    if at is None:
                        return
                    wait(pool, exp_done, at, SLOTS, g + 1, alone=True)
                    kind, n = T_GROUPS[g]
                    d = p1[at.u % 2][:, 4 * n:4 * n + 4, :] if kind == "k1" else p0[at.u % 2][:, 2 * n:2 * n + 2, 0:T]
                    pool.affine_select(out=d, in_=d, compare_op=ALU.is_ge, fill=0.0, base=0,
                                       pattern=[[0, 4 if kind == "k1" else 2], [1, T]], channel_multiplier=-1)\
                        .then_inc(masked, 1)

                def step(s):
                    i = s.image
                    causal(i(5), 2)
                    root_of(i(1), 0)
                    causal(i(5), 3)
                    rope_sum(i(2), 0)
                    affine(i(1))
                    causal(i(5), 4)
                    rope_sum(i(2), 1)
                    causal(i(5), 5)
                    root_of(i(1), 1)
                    causal(i(5), 6)
                    causal(i(5), 7)
                    root_of(i(6), 2)
                    causal(i(5), 8)
                    causal(i(4), 0)
                    causal(i(4), 1)
                run_steps(pool, step)


TABLE = 2 * ((TILES + 4 + 2 + 1) // 2)


def route(nc, sb, sem, psum, logits, lower, valid, lists, expert_in, scale_tiles, table):
    with ExitStack() as own:
        def buf(name, shape, dt=F32):
            return sb("r_" + name, shape, dt, own)

        G = SETS * NT
        top, total, pmax, other = (buf(n, [T, NT, SETS]) for n in ("top", "total", "pmax", "other"))
        prob, hot, wgt = (buf(n, [T, NT, ALL_E]) for n in ("prob", "hot", "wgt"))
        order = buf("order", [T, EXPERTS])
        base = buf("base", [T, ALL_E])
        valid_sb = buf("valid", [T, 2])
        lower_raw = buf("lower_raw", [T, T])
        lower_sb = buf("lower", [T, T], BF16)
        ones16 = buf("ones16", [T, T], BF16)
        ones = buf("ones", [T, NT])
        mask16 = buf("mask16", [T, NT, EXPERTS], BF16)
        tot = buf("tot", [T, EXPERTS, NT])
        incl = buf("incl", [T, EXPERTS, NT])
        pre = buf("pre", [T, NT, EXPERTS])
        work = buf("work", [T, NT, EXPERTS])
        keys = buf("keys", [T, NT, EXPERTS])
        above = buf("above", [T, NT, EXPERTS])
        dropped = buf("dropped", [T, NT])
        place = buf("place", [T, NT])
        pos_u32 = [buf("pos_common", [T, NT], U32), buf("pos_unique", [T, NT], U32)]
        ids = buf("ids", [T, NT], U32)
        cnt = buf("cnt", [T, EXPERTS])
        cnt16 = buf("cnt16", [T, EXPERTS], BF16)
        room = buf("room", [T, EXPERTS])
        thr, cand, gain = buf("thr", [T, EXPERTS]), buf("cand", [T, EXPERTS]), buf("gain", [T, EXPERTS])
        stepv = buf("stepv", [T, 1])
        number = buf("number", [T, ALL_E])
        empty = buf("empty", [128, LIST // 128], U32)
        num_i, tiles_i = buf("num_i", [1, ALL_E], I32), buf("tiles_i", [1, ALL_E], I32)
        tiles_f, cum, jump = buf("tiles_f", [1, ALL_E]), buf("cum", [1, ALL_E]), buf("jump", [1, ALL_E])
        slot_i = buf("slot_i", [1, TABLE], I32)
        slot_f, row_f, exp_f, ge_f, flag_f = (buf(n, [1, TABLE]) for n in ("slot_f", "row_f", "exp_f", "ge_f", "flag_f"))

        chain, const_in, pool_set, ids_done = sem("r_chain"), sem("r_const_in"), sem("r_pool_set"), sem("r_ids")
        exp_in, exp_out, mask_ready, prefix_done = sem("r_exp_in"), sem("r_exp_out"), sem("r_mask"), sem("r_prefix")
        cnt_ready, cnt_summed = sem("r_cnt"), sem("r_cnt_sum")
        b_cmp, b_cnt, b_mm, b_gain, b_thr, b_cand = (sem(f"r_b{n}") for n in ("cmp", "cnt", "mm", "gain", "thr", "cand"))
        pos_ready, lists_set, scattered, scales_out = sem("r_pos"), sem("r_lists_set"), sem("r_scat"), sem("r_scales")

        flat = "p t e -> p (t e)"
        bank_pre = psum[0:T, 0, :]
        bank_tot = psum[0:T, 1, :]
        bank_cnt = psum[0:T, 2, 0:EXPERTS]

        with nc.Block() as block:
            @block.sync
            def _(sp):
                sp.dma_start(valid_sb[:], valid).then_inc(const_in, 16)
                sp.dma_start(lower_raw[:], lower).then_inc(const_in, 16)
                sp.wait_ge(pool_set, 1)
                sp.dma_start(lists.rearrange("(p n) o -> p (n o)", p=128), empty[:]).then_inc(lists_set, 16)
                sp.wait_ge(scales_out, 1)
                sp.dma_start(expert_in.rearrange("(t p) c -> p t c", p=T)[:, :, C:SROW], scale_tiles[:])\
                    .then_inc(const_in, 16)
                sp.wait_ge(const_in, 48)

            @block.scalar
            def _(act):
                act.wait_ge(exp_in, 1)
                act.activation(prob[:], logits[:], ACT.Exp).then_inc(exp_out, 1)

            @block.gpsimd
            def _(pool):
                pool.memset(empty[:], EMPTY).then_inc(pool_set, 1)
                for e in range(EXPERTS):
                    pool.memset(order[:, e:e + 1], float(EXPERTS - e)).then_inc(pool_set, 1)
                for e in range(ALL_E):
                    pool.memset(base[:, e:e + 1], float(e * REGION)).then_inc(pool_set, 1)
                pool.memset(ones16[:], 1.0).then_inc(pool_set, 1)
                pool.memset(ones[:], 1.0).then_inc(pool_set, 1)
                pool.iota(ids[:], pattern=[[T, NT]], base=0, channel_multiplier=1).then_inc(pool_set, 1)
                pool.iota(slot_i[:], pattern=[[1, TABLE]], base=0, channel_multiplier=0).then_inc(pool_set, 1)
                pool.wait_ge(pool_set, 5 + ALL_E + 4)
                pool.wait_ge(lists_set, 16)
                for n in range(SETS):
                    pool.wait_ge(pos_ready, n + 1)
                    for t in range(NT):
                        pool.indirect_dma_start(lists, bass.IndirectOffsetOnAxis(ap=pos_u32[n][:, t:t + 1], axis=0),
                                                ids[:, t:t + 1], None, bounds_check=LIST - 1, oob_is_err=False)\
                            .then_inc(scattered, 16)
                pool.wait_ge(scattered, 16 * SETS * NT)

            @block.tensor
            def _(pe):
                pe.wait_ge(pool_set, 5 + ALL_E + 4)
                pe.wait_ge(const_in, 32)

                def prefix(n):
                    pe.wait_ge(mask_ready, n + 1)
                    m = mask16[:].rearrange(flat)
                    pe.matmul(bank_pre, lower_sb[:], m, start=True, stop=True)
                    pe.matmul(bank_tot, ones16[:], m, start=True, stop=True).then_inc(prefix_done, 1)

                prefix(0)
                with pe.Fori(0, BISECT) as i:
                    pe.wait_ge(b_cnt, i + 1)
                    pe.matmul(bank_cnt, ones16[:], cnt16[:], start=True, stop=True).then_inc(b_mm, 1)
                pe.wait_ge(cnt_ready, 1)
                pe.matmul(bank_cnt, ones16[:], cnt16[:], start=True, stop=True).then_inc(cnt_summed, 1)
                prefix(1)
                prefix(2)

            @block.vector
            def _(dve):
                links = [0]

                def link(ins):
                    links[0] += 1
                    ins.then_inc(chain, 1)
                    dve.wait_ge(chain, links[0])

                def four(ap):
                    return ap.rearrange("p t (s e) -> p (t s) e", s=SETS)

                def pairs(ap):
                    return ap[:].rearrange("p t s -> p (t s)")

                def over(ap):
                    return pairs(ap).unsqueeze(2).to_broadcast([T, G, EXPERTS])

                dve.wait_ge(pool_set, 5 + ALL_E + 4)
                dve.wait_ge(const_in, 32)
                dve.tensor_copy(lower_sb[:], lower_raw[:])
                link(dve.tensor_reduce(pairs(top), four(logits[:]), AX.X, ALU.max))
                dve.tensor_tensor(four(logits[:]), four(logits[:]), over(top), ALU.subtract).then_inc(exp_in, 1)
                dve.wait_ge(exp_out, 1)
                link(dve.tensor_reduce(pairs(total), four(prob[:]), AX.X, ALU.add))
                link(dve.reciprocal(pairs(total), pairs(total)))
                link(dve.tensor_tensor(four(prob[:]), four(prob[:]), over(total), ALU.mult))
                link(dve.tensor_reduce(pairs(pmax), four(prob[:]), AX.X, ALU.max))
                link(dve.reciprocal(pairs(other), pairs(pmax)))
                dve.tensor_tensor(scale_tiles[:], pmax[:], other[:], ALU.mult).then_inc(scales_out, 1)
                link(dve.tensor_tensor(four(wgt[:]), four(prob[:]), over(pmax), ALU.is_equal))
                link(dve.tensor_tensor(four(wgt[:]), four(wgt[:]), order[:].unsqueeze(1).to_broadcast([T, G, EXPERTS]),
                                       ALU.mult))
                link(dve.tensor_reduce(pairs(top), four(wgt[:]), AX.X, ALU.max))
                link(dve.tensor_tensor(four(hot[:]), four(wgt[:]), over(top), ALU.is_equal))
                ok = valid_sb[:].unsqueeze(1).to_broadcast([T, IMAGES, 2])
                for e in range(ALL_E):
                    h = hot[:, :, e].rearrange("p (b t) -> p b t", t=2)
                    ins = dve.tensor_tensor(h, h, ok, ALU.mult)
                link(ins)
                hot_c, hot_u = hot[:, :, 0:EXPERTS], hot[:, :, EXPERTS:ALL_E]

                def ranks(n, mask):
                    dve.tensor_copy(mask16[:], mask).then_inc(mask_ready, 1)
                    dve.wait_ge(prefix_done, n + 1)
                    link(dve.tensor_copy(tot[:], bank_tot.rearrange("p (t e) -> p e t", e=EXPERTS)))
                    for e in range(EXPERTS):
                        ins = dve.tensor_tensor_scan(incl[:, e, :], ones[:], tot[:, e, :], 0.0, ALU.mult, ALU.add)
                    link(ins)
                    link(dve.tensor_tensor(tot[:], incl[:], tot[:], ALU.subtract))
                    link(dve.tensor_tensor(pre[:], bank_pre.rearrange("p (t e) -> p t e", e=EXPERTS),
                                           tot[:].rearrange("p e t -> p t e"), ALU.add))

                def positions(n, mask, member):
                    link(dve.tensor_copy(number[:, n * EXPERTS:(n + 1) * EXPERTS], incl[:, :, NT - 1]))
                    b = base[:, n * EXPERTS:(n + 1) * EXPERTS].unsqueeze(1).to_broadcast([T, NT, EXPERTS])
                    link(dve.tensor_tensor(work[:], pre[:], b, ALU.add))
                    link(dve.tensor_tensor(work[:], work[:], mask, ALU.mult))
                    link(dve.tensor_reduce(place[:], work[:], AX.X, ALU.add))
                    link(dve.tensor_scalar(work[:, :, 0], member, -float(EMPTY), float(EMPTY), ALU.mult, ALU.add))
                    dve.tensor_tensor(pos_u32[n][:], place[:], work[:, :, 0], ALU.add).then_inc(pos_ready, 1)

                ranks(0, hot_c)
                link(dve.tensor_reduce(dropped[:], hot_c, AX.X, ALU.add))
                positions(0, hot_c, dropped[:])

                link(dve.memset(thr[:], 0.0))
                pm = pmax[:, :, 0].unsqueeze(2).to_broadcast([T, NT, EXPERTS])
                dve.wait_ge(pos_ready, 1)
                link(dve.tensor_scalar(work[:], hot_c, 1.0, None, ALU.subtract))
                link(dve.tensor_tensor(keys[:], hot_c, pm, ALU.mult))
                link(dve.tensor_tensor(keys[:], keys[:], work[:], ALU.add))
                link(dve.memset(stepv[:], 0.5))
                dve.memset(cand[:], 0.5).then_inc(b_cand, 1)
                with dve.Fori(0, BISECT) as i:
                    dve.wait_ge(b_cand, i + 1)
                    dve.tensor_tensor(above[:], keys[:], cand[:].unsqueeze(1).to_broadcast([T, NT, EXPERTS]), ALU.is_ge)\
                        .then_inc(b_cmp, 1)
                    dve.wait_ge(b_cmp, i + 1)
                    with nc.allow_low_precision("a count up to 128 is exact in bfloat16"):
                        dve.tensor_reduce(cnt16[:], above[:].rearrange("p t e -> p e t"), AX.X, ALU.add)\
                            .then_inc(b_cnt, 1)
                    dve.wait_ge(b_mm, i + 1)
                    dve.tensor_scalar(gain[:], bank_cnt, float(CAPACITY), stepv[:, 0:1], ALU.is_ge, ALU.mult)\
                        .then_inc(b_gain, 1)
                    dve.wait_ge(b_gain, i + 1)
                    dve.tensor_tensor(thr[:], thr[:], gain[:], ALU.add)
                    dve.tensor_scalar(stepv[:], stepv[:], 0.5, None, ALU.mult).then_inc(b_thr, 1)
                    dve.wait_ge(b_thr, i + 1)
                    dve.tensor_scalar(cand[:], thr[:], stepv[:, 0:1], None, ALU.add).then_inc(b_cand, 1)

                t4 = thr[:].unsqueeze(1).to_broadcast([T, NT, EXPERTS])
                link(dve.tensor_tensor(above[:], keys[:], t4, ALU.is_gt))
                with nc.allow_low_precision("a count up to 128 is exact in bfloat16"):
                    dve.tensor_reduce(cnt16[:], above[:].rearrange("p t e -> p e t"), AX.X, ALU.add).then_inc(cnt_ready, 1)
                dve.wait_ge(cnt_summed, 1)
                link(dve.tensor_scalar(room[:], bank_cnt, -1.0, float(CAPACITY), ALU.mult, ALU.add))
                link(dve.tensor_tensor(keys[:], keys[:], t4, ALU.is_equal))
                ranks(1, keys[:])
                link(dve.tensor_tensor(work[:], pre[:], room[:].unsqueeze(1).to_broadcast([T, NT, EXPERTS]), ALU.is_lt))
                link(dve.tensor_tensor(work[:], work[:], keys[:], ALU.mult))
                link(dve.tensor_tensor(work[:], work[:], above[:], ALU.add))
                link(dve.tensor_tensor(work[:], hot_c, work[:], ALU.subtract))
                link(dve.tensor_reduce(dropped[:], work[:], AX.X, ALU.max))
                link(dve.tensor_tensor(hot_u, hot_u, dropped[:].unsqueeze(2).to_broadcast([T, NT, EXPERTS]), ALU.mult))
                ranks(2, hot_u)
                positions(1, hot_u, dropped[:])

                link(dve.tensor_scalar(num_i[:], number[0:1, :], float(TS - 1), None, ALU.add))
                link(dve.tensor_scalar(tiles_i[:], num_i[:], TS.bit_length() - 1, None, ALU.arith_shift_right))
                link(dve.tensor_copy(tiles_f[:], tiles_i[:]))
                link(dve.tensor_tensor_scan(cum[:], ones[0:1, 0:ALL_E], tiles_f[:], 0.0, ALU.mult, ALU.add))
                link(dve.tensor_scalar(jump[:], tiles_f[:], -float(TS), float(REGION), ALU.mult, ALU.add))
                link(dve.tensor_copy(slot_f[:], slot_i[:]))
                link(dve.tensor_scalar(row_f[:], slot_f[:], float(TS), None, ALU.mult))
                link(dve.memset(exp_f[:], 0.0))
                for e in range(ALL_E - 1):
                    link(dve.tensor_scalar(ge_f[:], slot_f[:], cum[:, e:e + 1], None, ALU.is_ge))
                    link(dve.tensor_tensor(exp_f[:], exp_f[:], ge_f[:], ALU.add))
                    link(dve.tensor_scalar(ge_f[:], ge_f[:], jump[:, e:e + 1], None, ALU.mult))
                    link(dve.tensor_tensor(row_f[:], row_f[:], ge_f[:], ALU.add))
                link(dve.tensor_scalar(ge_f[:], slot_f[:], cum[:, ALL_E - 1:ALL_E], None, ALU.is_ge))
                link(dve.tensor_scalar(flag_f[:], row_f[:], -1.0, float(NULL_AT), ALU.mult, ALU.add))
                link(dve.tensor_tensor(flag_f[:], flag_f[:], ge_f[:], ALU.mult))
                link(dve.tensor_tensor(row_f[:], row_f[:], flag_f[:], ALU.add))
                link(dve.tensor_copy(table[:, 0:TABLE], row_f[:]))
                link(dve.tensor_copy(table[:, TABLE:2 * TABLE], exp_f[:]))
                link(dve.memset(flag_f[:], 1.0))
                link(dve.tensor_tensor(flag_f[:, 2:TABLE], exp_f[:, 2:TABLE], exp_f[:, 0:TABLE - 2], ALU.not_equal))
                link(dve.tensor_copy(table[:, 2 * TABLE:3 * TABLE], flag_f[:]))
                link(dve.tensor_scalar(flag_f[:], exp_f[:], float(EXPERTS), None, ALU.is_ge))
                link(dve.tensor_copy(table[:, 3 * TABLE:4 * TABLE], flag_f[:]))
                link(dve.tensor_copy(table[:, 4 * TABLE:4 * TABLE + 1], cum[:, ALL_E - 1:ALL_E]))
                link(dve.tensor_scalar(num_i[:, 0:1], cum[:, ALL_E - 1:ALL_E], 3.0, None, ALU.add))
                link(dve.tensor_scalar(table[:, 4 * TABLE + 1:4 * TABLE + 2], num_i[:, 0:1], 1, None,
                                       ALU.arith_shift_right))


class Tile:

    def __init__(self, w, p):
        self.w, self.p = w, p
        self.static = isinstance(w, int)
        self.n = w * 2 + p


def experts(nc, sb, sem, psum, identity, table, lists, expert_in, w1_parts, w2_parts, b1, b2, out):
    LAGS = 4
    PAIRS = TABLE // 2
    with ExitStack() as own:
        def two(name, shape, dt=F32):
            return [sb(f"e_{name}{i}", shape, dt, own) for i in range(2)]

        w1b, w2b = two("w1", [CH, 2, 2, HID], F32R), two("w2", [128, 2, FT, C], F32R)
        b1b, b2b = two("b1", [128, FT]), two("b2", [128, C])
        idx_in, idx_out = two("idx_in", [128, 2], U32), two("idx_out", [128, 2], U32)
        rows = two("rows", [128, 2, SROW])
        scale = two("scale", [128, 2])
        xt = [two("xt_hi", [CH, 2, TS], F32R), two("xt_lo", [CH, 2, TS], F32R)]
        act_f = two("act", [128, FT, TS])
        act_p = [two("act_hi", [128, FT, TS], F32R), two("act_lo", [128, FT, TS], F32R)]
        ysum = sb("e_ysum", [128, 2, C], F32, own)
        y = two("y", [128, 2, C])

        def twos(name):
            return [sem(f"e_{name}{i}") for i in range(2)]

        rows_set = sem("e_rows_set")
        idx_loaded, idx_again, w_loaded, gathered, scattered = (
            twos("idx_loaded"), twos("idx_again"), twos("w_loaded"), twos("gathered"), twos("scattered"))
        turned, xhi, xlo = sem("e_turned"), sem("e_xhi"), sem("e_xlo")
        l1, gelu, ahi, alo, l2, ysummed, ydone, kept = (
            sem("e_" + n) for n in ("l1", "gelu", "ahi", "alo", "l2", "ysummed", "ydone", "kept"))

        turn_bank = [psum[:, 0, :], psum[:, 1, :]]
        l1_bank = [psum[:, 2 + k, :].rearrange("p (f t) -> p f t", f=2) for k in range(3)]
        l2_bank = [psum[:, 5 + i, 0:2 * C].rearrange("p (n c) -> p n c", n=2) for i in range(2)]

        def since(eng, s, tile, per, add):
            if tile.static:
                if per * tile.n + add > 0:
                    eng.wait_ge(s, per * tile.n + add)
            else:
                reg_wait(eng, s, tile.w * (2 * per) + (per * tile.p + add), eng.engine == mybir.EngineType.Pool)

        def landed(eng, s, tile, per, back=0):
            if tile.static:
                if tile.w + 1 - back > 0:
                    eng.wait_ge(s[tile.p], per * (tile.w + 1 - back))
            else:
                reg_wait(eng, s[tile.p], tile.w * per + per * (1 - back), eng.engine == mybir.EngineType.Pool)

        def run(eng, body):
            def pair(k):
                for p in range(2):
                    def tile(lag):
                        if isinstance(k, int) and 2 * k + p < lag:
                            return None
                        return Tile(k + (p - lag) // 2, (p - lag) % 2)
                    body(tile)
            for k in range(LAGS // 2 + 1):
                pair(k)
            count = eng.value_load(table[0:1, 4 * TABLE:4 * TABLE + 1], min_val=0, max_val=TILES)
            with eng.Fori(LAGS // 2 + 1, PAIRS) as k:
                with eng.If(k * 2 < count + (LAGS + 2)):
                    pair(k)
            return eng.value_load(table[0:1, 4 * TABLE + 1:4 * TABLE + 2], min_val=1, max_val=PAIRS)

        def entry(eng, tile, column, most):
            return eng.value_load(table[0:1, bass.ds(tile.n + column * TABLE, 1)], min_val=0, max_val=most)

        with nc.Block() as block:
            @block.sync
            def _(sp):
                def indices(tile, dst, free, done, back):
                    if tile is None:
                        return
                    landed(sp, free, tile, 32, back)
                    row = entry(sp, tile, 0, NULL_AT)
                    sp.dma_start(dst[tile.p][:], lists[bass.ds(row, TS)].rearrange("(p n) o -> p (n o)", n=2))\
                        .then_inc(done[tile.p], 16)

                def weights(tile):
                    if tile is None:
                        return
                    since(sp, l2, tile, 1, -1)
                    since(sp, ydone, tile, 1, -1)
                    e = entry(sp, tile, 1, ALL_E - 1)
                    new = entry(sp, tile, 2, 1) > 0
                    p = tile.p
                    sp.dma_start(w1b[p][:].bitcast(F32).rearrange("p a c n -> p (a c n)"),
                                 w1_parts[bass.ds(e, 1)].rearrange("e p n -> (e p) n"), cond=new).then_inc(w_loaded[p], 16)
                    sp.dma_start(w2b[p][:].bitcast(F32).rearrange("p a c n -> p (a c n)"),
                                 w2_parts[bass.ds(e, 1)].rearrange("e p n -> (e p) n"), cond=new).then_inc(w_loaded[p], 16)
                    sp.dma_start(b1b[p][:], b1[bass.ds(e, 1)].rearrange("e p n -> (e p) n"), cond=new)\
                        .then_inc(w_loaded[p], 16)
                    sp.dma_start(b2b[p][:], b2[bass.ds(e, 1)].rearrange("e p n -> (e p) n"), cond=new)\
                        .then_inc(w_loaded[p], 16)

                def body(tile):
                    indices(tile(0), idx_in, gathered, idx_loaded, 1)
                    weights(tile(1))
                    indices(tile(3), idx_out, scattered, idx_again, 1)
                more = run(sp, body)
                for i in range(2):
                    reg_wait(sp, idx_loaded[i], more * 16 + 32)
                    reg_wait(sp, w_loaded[i], more * 64 + 64 * (2 - i))
                    reg_wait(sp, idx_again[i], more * 16 + 16 * (1 - i))

            @block.gpsimd
            def _(pool):
                for i in range(2):
                    pool.memset(rows[i][:], 0.0).then_inc(rows_set, 1)
                pool.wait_ge(rows_set, 2)

                def gather(tile):
                    if tile is None:
                        return
                    landed(pool, idx_loaded, tile, 16)
                    since(pool, turned, tile, 1, -1)
                    since(pool, kept, tile, 1, -1)
                    for n in range(2):
                        pool.indirect_dma_start(rows[tile.p][:, n, :], None, expert_in,
                                                bass.IndirectOffsetOnAxis(ap=idx_in[tile.p][:, n:n + 1], axis=0),
                                                bounds_check=NROW - 1, oob_is_err=False).then_inc(gathered[tile.p], 16)

                def scatter(tile):
                    if tile is None:
                        return
                    landed(pool, idx_again, tile, 16)
                    since(pool, ydone, tile, 1, 1)
                    before = Tile(tile.w - 1 + tile.p, 1 - tile.p)
                    landed(pool, scattered, before, 32)
                    for n in range(2):
                        pool.indirect_dma_start(out, bass.IndirectOffsetOnAxis(ap=idx_out[tile.p][:, n:n + 1], axis=0),
                                                y[tile.p][:, n, :], None, bounds_check=NROW - 1, oob_is_err=False,
                                                compute_op=ALU.add).then_inc(scattered[tile.p], 16)

                def body(tile):
                    gather(tile(0))
                    scatter(tile(4))
                more = run(pool, body)
                for i in range(2):
                    reg_wait(pool, gathered[i], more * 32 + 64, True)
                    reg_wait(pool, scattered[i], more * 32, True)
                pool.drain()

            @block.tensor
            def _(pe):
                def turn(tile):
                    if tile is None:
                        return
                    landed(pe, gathered, tile, 32)
                    since(pe, xlo, tile, 1, -1)
                    for n in range(2):
                        for c in range(2):
                            mm = pe.transpose(turn_bank[tile.p][0:CH, c * TS + n * 128:c * TS + (n + 1) * 128],
                                              rows[tile.p][:, n, c * CH:(c + 1) * CH], identity[:])
                    mm.then_inc(turned, 1)

                def layer1(tile):
                    if tile is None:
                        return
                    since(pe, xlo, tile, 1, 1)
                    landed(pe, w_loaded, tile, 64)
                    w, x_ = w1b[tile.p], [xt[a][tile.p] for a in range(2)]
                    for k in range(3):
                        since(pe, gelu, tile, 3, k - 2)
                        for i in range(2):
                            f = slice((2 * k + i) * 128, (2 * k + i + 1) * 128)
                            for c in range(2):
                                mm = split3(pe, l1_bank[k][:, i, :], w[:, 0, c, f], w[:, 1, c, f], x_[0][:, c, :],
                                            x_[1][:, c, :], c == 0, c == 1)
                        mm.then_inc(l1, 1)

                def layer2(tile):
                    if tile is None:
                        return
                    since(pe, ydone, tile, 1, -1)
                    since(pe, alo, tile, 3, 3)
                    p = tile.p
                    for n in range(2):
                        s = slice(n * 128, (n + 1) * 128)
                        for f in range(FT):
                            mm = split3(pe, l2_bank[p][:, n, :], act_p[0][p][:, f, s], act_p[1][p][:, f, s],
                                        w2b[p][:, 0, f, :], w2b[p][:, 1, f, :], f == 0, f == FT - 1)
                    mm.then_inc(l2, 1)

                def body(tile):
                    turn(tile(1))
                    layer1(tile(2))
                    layer2(tile(3))
                run(pe, body)

            @block.scalar
            def _(act):
                def x_hi(tile):
                    if tile is None:
                        return
                    since(act, turned, tile, 1, 1)
                    since(act, l1, tile, 3, -3)
                    act.copy(xt[0][tile.p][:].rearrange("p c t -> p (c t)"), turn_bank[tile.p][0:CH, :]).then_inc(xhi, 1)

                def gelus(tile):
                    if tile is None:
                        return
                    since(act, alo, tile, 3, -3)
                    for k in range(3):
                        since(act, l1, tile, 3, k + 1)
                        for i in range(2):
                            f = 2 * k + i
                            ins = act.activation(act_f[tile.p][:, f, :], l1_bank[k][:, i, :], ACT.Gelu,
                                                 bias=b1b[tile.p][:, f:f + 1])
                        ins.then_inc(gelu, 1)

                def body(tile):
                    x_hi(tile(1))
                    gelus(tile(2))
                run(act, body)

            @block.vector
            def _(dve):
                def keep(tile):
                    if tile is None:
                        return
                    landed(dve, gathered, tile, 32)
                    since(dve, ydone, tile, 1, -1)
                    unique = entry(dve, tile, 3, 1)
                    dve.tensor_copy(scale[tile.p][:], rows[tile.p][:, :, bass.ds(unique + C, 1)]
                                    .rearrange("p n o -> p (n o)")).then_inc(kept, 1)

                def x_lo(tile):
                    if tile is None:
                        return
                    since(dve, xhi, tile, 1, 1)
                    dve.tensor_tensor(xt[1][tile.p][:].rearrange("p c t -> p (c t)"), turn_bank[tile.p][0:CH, :],
                                      xt[0][tile.p][:].bitcast(F32).rearrange("p c t -> p (c t)"), ALU.subtract)\
                        .then_inc(xlo, 1)

                def parts(tile):
                    if tile is None:
                        return
                    since(dve, l2, tile, 1, -1)
                    p = tile.p
                    for k in range(3):
                        since(dve, gelu, tile, 3, k + 1)
                        f = slice(2 * k, 2 * k + 2)
                        dve.tensor_copy(act_p[0][p][:, f, :], act_f[p][:, f, :]).then_inc(ahi, 1)
                        since(dve, ahi, tile, 3, k + 1)
                        dve.tensor_tensor(act_p[1][p][:, f, :], act_f[p][:, f, :], act_p[0][p][:, f, :].bitcast(F32),
                                          ALU.subtract).then_inc(alo, 1)

                def result(tile):
                    if tile is None:
                        return
                    since(dve, l2, tile, 1, 1)
                    landed(dve, scattered, tile, 32, 1)
                    p = tile.p
                    dve.tensor_tensor(ysum[:], l2_bank[p], b2b[p][:].unsqueeze(1).to_broadcast([128, 2, C]), ALU.add)\
                        .then_inc(ysummed, 1)
                    since(dve, ysummed, tile, 1, 1)
                    for n in range(2):
                        ins = dve.tensor_scalar(y[p][:, n, :], ysum[:, n, :], scale[p][:, n:n + 1], None, ALU.mult)
                    ins.then_inc(ydone, 1)

                def body(tile):
                    result(tile(3))
                    keep(tile(1))
                    x_lo(tile(1))
                    parts(tile(2))
                run(dve, body)


_DEVICE = [("x", (IMAGES, 128, KIN, ROWS)), ("w_emb", (128, KIN, C)), ("tok_rows", (T, 2, C)), ("pos", (T, 2, C)),
           ("gamma", (C,)), ("beta", (C,)), ("w_qk", (CH, 2, 2 * C)), ("w_v", (CH, 2, C)), ("w_proj", (CH, 2, C)),
           ("w_router", (CH, 2, ALL_E)), ("b_router", (ALL_E,)), ("cos", (T, 2, D)), ("sin", (T, 2, D)),
           ("ident", (128, 128)), ("tri", (T, 4, T)), ("lower", (T, T)), ("w1", (ALL_E, CH, W1C)),
           ("w2", (ALL_E, 128, W2C)), ("b1", (ALL_E, 128, FT)), ("b2", (ALL_E, 128, C)), ("valid", (T, 2))]


def _tiles(rows):
    return np.ascontiguousarray(rows.reshape(2, T, -1).transpose(1, 0, 2))


def _constants():
    i = np.arange(TOKENS, dtype=np.float32)[:, None]
    j = np.arange(C, dtype=np.float32)[None, :]
    angle = (i / np.power(np.float32(10000.0), np.floor(j / 2.0) * 2.0 / C)).astype(np.float32)
    pos = np.zeros((ROWS, C), np.float32)
    pos[:TOKENS] = np.where(np.arange(C)[None, :] % 2 == 0, np.sin(angle), np.cos(angle))
    inv = (1.0 / np.float32(10000.0) ** (np.arange(0, D, 2, dtype=np.float32) / D)).astype(np.float32)
    ang = np.arange(ROWS, dtype=np.float32)[:, None] * inv[None, :]
    cos = np.concatenate([np.cos(ang)] * 2, axis=1)
    sin = np.concatenate([-np.sin(ang), np.sin(ang)], axis=1)
    q = np.arange(T)
    tri = np.where(q[None, :] > q[:, None], -1e30, 0.0).astype(np.float32)
    valid = np.ones((T, 2), np.float32)
    valid[TOKENS - T:, 1] = 0.0
    return dict(pos=_tiles(pos), cos=_tiles(cos.astype(np.float32)), sin=_tiles(sin.astype(np.float32)),
                ident=np.eye(128, dtype=np.float32), tri=np.repeat(tri[:, None, :], 4, axis=1),
                lower=np.triu(np.ones((T, T), np.float32), 1), valid=valid)


def _halves(w):
    return np.ascontiguousarray(w.reshape(2, CH, -1).transpose(1, 0, 2))


def _layout(a):
    a = {k: np.asarray(v) for k, v in a.items()}
    img = a["x"].reshape(IMAGES, 3, PATCHES, PIX, PATCHES, PIX).transpose(0, 1, 3, 5, 2, 4)
    img = img.reshape(IMAGES, KIN, 128, PATCHES * PATCHES)
    x = np.zeros((IMAGES, 128, KIN, ROWS), np.float32)
    x[..., 1:TOKENS] = img.transpose(0, 2, 1, 3)
    rows = np.empty((ROWS, C), np.float32)
    rows[:] = a["L0_tok_b"]
    rows[0] = a["L0_tok_class_token"][0]
    w_qkv = a["L0_attn_w_qkv"]
    w1 = np.concatenate([a["L0_ffn_W1c"], a["L0_ffn_W1u"]])
    w2 = np.concatenate([a["L0_ffn_W2c"], a["L0_ffn_W2u"]])
    b1 = np.concatenate([a["L0_ffn_b1c"], a["L0_ffn_b1u"]])
    b2 = np.concatenate([a["L0_ffn_b2c"], a["L0_ffn_b2u"]])
    return dict(
        _constants(), x=x, w_emb=a["L0_tok_W"].T.reshape(KIN, 128, C).transpose(1, 0, 2), tok_rows=_tiles(rows),
        gamma=a["L0_tok_gamma"], beta=a["L0_tok_beta"], w_qk=_halves(w_qkv[:2 * C].T), w_v=_halves(w_qkv[2 * C:].T),
        w_proj=_halves(a["L0_attn_w_proj"].T),
        w_router=_halves(np.concatenate([a["L0_ffn_Wsc"], a["L0_ffn_Wsu"]], axis=1)),
        b_router=np.concatenate([a["L0_ffn_bsc"], a["L0_ffn_bsu"]]),
        w1=w1.reshape(ALL_E, 2, CH, HID).transpose(0, 2, 1, 3).reshape(ALL_E, CH, W1C),
        w2=w2.reshape(ALL_E, FT, 128, C).transpose(0, 2, 1, 3).reshape(ALL_E, 128, W2C),
        b1=b1.reshape(ALL_E, FT, 128).transpose(0, 2, 1), b2=np.repeat(b2[:, None, :], 128, axis=1))


def kernel(**inputs):
    import concourse.bacc as bacc
    from concourse.bass_utils import run_bass_kernel_spmd

    nc = bacc.Bacc("TRN2", target_bir_lowering=False, num_devices=1)
    given = _layout(inputs)
    arrays, args = {}, []
    for name, shape in _DEVICE:
        a = np.ascontiguousarray(given[name])
        assert a.shape == shape, (name, a.shape)
        arrays[f"in_{name}"] = a
        args.append(nc.dram_tensor(f"in_{name}", shape, mybir.dt.from_np(a.dtype), kind="ExternalInput").ap())
    args.append(nc.dram_tensor("out_rows", (NROW, C), F32, kind="ExternalOutput").ap())
    program(nc, *args)
    r = run_bass_kernel_spmd(nc, [arrays], core_ids=[0])
    got = r.results[0]["out_rows"]
    return np.ascontiguousarray(got.reshape(IMAGES, ROWS, C)[:, :TOKENS])
```

```python
from contextlib import ExitStack

import numpy as np

import concourse.bass as bass
from concourse import mybir

F32 = mybir.dt.float32
F32R = mybir.dt.float32r
BF16 = mybir.dt.bfloat16
I32 = mybir.dt.int32
U32 = mybir.dt.uint32
ALU = mybir.AluOpType
ACT = mybir.ActivationFunctionType
AX = mybir.AxisListType

IMAGES = 64
PATCHES = 14
PIX = 16
TOKENS = PATCHES * PATCHES + 1
T = 100
ROWS = 2 * T
C = 192
KIN = 3 * PIX * PIX // 128
HEADS = 12
D = C // HEADS
CH = C // 2
HID = 768
FT = HID // 128
EXPERTS = 4
SETS = 2
ALL_E = SETS * EXPERTS
NROW = IMAGES * ROWS
NTOK = IMAGES * TOKENS
CAPACITY = NTOK // EXPERTS
NT = 2 * IMAGES
EPS = 1e-5

PARTS = 3
KS = PARTS * D
KP = 127
MROW = KP

TS = 256
REGION = (NROW + TS - 1) // TS * TS
NULL_AT = EXPERTS * REGION
LIST = NULL_AT + TS
EMPTY = 1 << 20
TILES_C = (NTOK + EXPERTS * (TS - 1)) // TS
TILES_U = (NTOK - CAPACITY + EXPERTS * (TS - 1)) // TS
LEAST_C = (NTOK + TS - 1) // TS
TABLE = 2 * ((max(TILES_C, TILES_U) + 7) // 2)
COLUMNS = 3 * TABLE + 2
SCATTERS = NROW // 128
BISECT = 26

WC = 2 * C
Q1, Q2 = 2 * HID // WC, FT * C // WC
QE = Q1 + Q2
SROW = C + SETS

SLOTS = 9
TAU = dict(E0=7, E1=8, STATS1=9, NORM1=10, STATS2=12, NORM2=13, N1T=16, QK0=18, QK1=19, V=20, QT0=22, QT1=23,
           S=29, MT=39, TG=43, PV=46, ONORM=54, ATT=55, PROJ=58, NORM3=60, N2T=62, LG=68)
MISC = ("N1T", "V", "MT", "ATT", "PROJ", "N2T", "LG")
LAST = max(TAU.values()) // SLOTS
UNROLL = 4
LOOP_FROM = 8
LOOP_TO = IMAGES
assert LOOP_TO - LOOP_FROM == ALL_E * QE

T_GROUPS = [("k1", 0), ("k0", 0), ("k0", 1), ("k1", 1), ("k0", 2), ("k0", 3), ("k1", 2), ("k0", 4), ("k0", 5)]
PAIR_GROUP = [T_GROUPS.index(("k0", p)) for p in range(6)]


class At:

    def __init__(self, n, u):
        self.n, self.u = n, u % UNROLL
        self.static = isinstance(n, int)

    def times(self, k, add):
        return self.n * k + add if self.static or k != 1 else self.n + add


class Step:
    def __init__(self, n, c):
        self.n, self.c = n, c
        self.static = isinstance(n, int)

    def image(self, lag):
        if self.static:
            j = self.n - lag
            return At(j, j) if 0 <= j < IMAGES else None
        return At(self.n - lag, self.c - lag)


started = []


def reg_wait(eng, sem, value, alone=False):
    if alone or eng.engine == mybir.EngineType.SP:
        value = eng.to_reg(value)
        eng.wait_ge(started[0], 16)
    eng.wait_ge(sem, value)


def wait(eng, sem, at, k, add, most=None, alone=False):
    v = at.times(k, add)
    if at.static:
        if most is not None:
            v = min(v, most)
        if v > 0:
            eng.wait_ge(sem, v)
    else:
        reg_wait(eng, sem, v, alone)


def run_steps(eng, body):
    for s in range(LOOP_FROM):
        body(Step(s, s))
    with eng.Fori(0, (LOOP_TO - LOOP_FROM) // UNROLL) as it:
        for c in range(UNROLL):
            body(Step(it * UNROLL + (LOOP_FROM + c), LOOP_FROM + c))
    for s in range(LOOP_TO, IMAGES + LAST):
        body(Step(s, s))


def misc_uses(step, slot):
    return sum(min(max(step - TAU[x] // SLOTS + (TAU[x] % SLOTS <= slot), 0), IMAGES) for x in MISC)


def misc_count(at, use):
    lag, slot = TAU[use] // SLOTS, TAU[use] % SLOTS
    if at.static:
        return 0, misc_uses(at.n + lag, slot)
    mid = IMAGES // 2
    k = len(MISC)
    return k, misc_uses(mid + lag, slot) - k * mid


def split3(eng, out, a_hi, a_lo, b_hi, b_lo, first, last):
    eng.matmul(out, a_hi, b_hi, start=first, stop=False)
    eng.matmul(out, a_hi, b_lo, start=False, stop=False)
    return eng.matmul(out, a_lo, b_hi, start=False, stop=last)


def program(nc, x, w_emb, tok_rows, pos, gamma, beta, w_qk, w_v, w_proj, w_router, b_router, cos, sin, ident, tri,
            lower, w_experts, b1, b2, valid, out):
    ctx = ExitStack()
    with ctx:
        def sb(name, shape, dt=F32, where=ctx):
            return where.enter_context(nc.sbuf_tensor("s_" + name, shape, dt))

        def sem(name):
            return ctx.enter_context(nc.semaphore(name))

        psum = ctx.enter_context(nc.psum_tensor("psum", [128, 8, 512], F32))
        expert_in = nc.dram_tensor("expert_in", [NROW, SROW], F32, kind="Internal").ap()
        w_parts = nc.dram_tensor("w_parts", [ALL_E * QE, 128, 2 * WC], F32, kind="Internal").ap()
        lists = [nc.dram_tensor(f"lists{i}", [LIST, 1], U32, kind="Internal").ap() for i in range(SETS)]
        logits = sb("logits", [T, NT, ALL_E])
        identity = sb("identity", [128, 128])

        started[:] = [sem("started")]

        attention(nc, sb, sem, psum, x, w_emb, tok_rows, pos, gamma, beta, w_qk, w_v, w_proj, w_router, b_router,
                  cos, sin, tri, ident, w_experts, identity, logits, expert_in, w_parts, out)
        scale_tiles = sb("scale_tiles", [T, NT, SETS])
        tables = sb("tables", [1, SETS * COLUMNS], I32)
        place_id = [sb(f"place_id{i}", [128, 2 * TABLE, 2], U32) for i in range(SETS)]
        route(nc, sb, sem, psum, logits, lower, valid, lists, expert_in, scale_tiles, tables, place_id)
        for n in range(SETS):
            experts(nc, sb, sem, psum, n, identity, tables, lists, place_id, expert_in, w_parts, b1, b2, out)


def attention(nc, sb, sem, psum, x, w_emb, tok_rows, pos, gamma, beta, w_qk, w_v, w_proj, w_router, b_router,
              cos, sin, tri, ident, w_experts, identity, logits, expert_in, w_parts, out):
    with ExitStack() as own:
        used = []

        def sem(name):
            used.append(own.enter_context(nc.semaphore(name)))
            return used[-1]

        def buf(name, shape, dt=F32):
            return sb(name, shape, dt, own)

        first = buf("first", [1, 1])
        wemb = [buf("wemb_hi", [128, KIN, C], F32R), buf("wemb_lo", [128, KIN, C], F32R)]
        table = buf("tok_table", [T, 2, C])
        gamma_sb = buf("gamma", [T, C])
        beta_sb = buf("beta", [T, C])
        br_sb = buf("b_router", [T, ALL_E])
        cos_sb = buf("cos", [T, 2, D])
        sin_sb = buf("sin", [T, 2, D])
        tri_sb = buf("tri_sb", [T, 4, T], BF16)
        eye16 = buf("eye16", [T, T], BF16)
        logits_lo = buf("logits_lo", [T, 2, ALL_E])
        half = buf("minus_half", [T, 2])
        router_w = buf("router_w", [128, 2, 2 * ALL_E], F32R)
        whi = buf("w_hi", [128, 2, 3 * C + C + ALL_E], F32R)
        wlo = buf("w_lo", [128, 2, 3 * C + C + ALL_E], F32R)
        QK, VV, PJ, RT = (slice(0, 2 * C), slice(2 * C, 3 * C), slice(3 * C, 4 * C), slice(4 * C, 4 * C + ALL_E))

        x_in = buf("x_in", [128, KIN, ROWS])
        x_hi, x_lo = buf("x_hi", [128, KIN, ROWS], F32R), buf("x_lo", [128, KIN, ROWS], F32R)
        xs = buf("xs", [T, 2, C])
        xn = buf("xn", [T, 2, C])
        h_new = [buf(f"h_new{i}", [T, 2, C]) for i in range(2)]
        h_old = [buf(f"h_old{i}", [T, 2, C]) for i in range(2)]
        stat = [buf(f"stat{i}", [T, 2, 6]) for i in range(3)]
        mv = [buf(f"mv{i}", [T, 2, 2]) for i in range(3)]
        var_eps = [buf(f"var_eps{i}", [T, 2]) for i in range(3)]
        rstd = [buf(f"rstd{i}", [T, 2]) for i in range(3)]
        n1 = buf("n1", [T, 2, C])
        n1t = [buf(f"n1t_{a}", [128, 2, ROWS], F32R) for a in ("hi", "lo")]
        roped = [buf(f"rope_cos{i}", [T, 2 * C]) for i in range(2)]
        ropes = [buf(f"rope_sin{i}", [T, 2 * C]) for i in range(2)]
        qkr = buf("qk_rot", [T, 2, 2 * C])
        v_aug = [buf(f"v_aug{i}", [T, 2, HEADS, D + 1]) for i in range(4)]
        qkt = [buf("qkt_hi", [CH, 4, ROWS], F32R), buf("qkt_lo", [CH, 4, ROWS], F32R)]
        q_st = [buf(f"q_stack{i}", [KP + 1, HEADS, ROWS], F32R) for i in range(4)]
        k_st = [buf(f"k_stack{i}", [KP + 1, HEADS, ROWS], F32R) for i in range(4)]
        rmax = [buf(f"row_max{i}", [T, 2, HEADS]) for i in range(2)]
        rmax_t = buf("row_max_t", [HEADS, ROWS], F32R)
        p0_all = [buf(f"p_k0_{i}", [128, HEADS, ROWS]) for i in range(2)]
        p0 = [p[0:T] for p in p0_all]
        raw = p0_all[0][0:CH].rearrange("p a b -> p (a b)")[:, 0:2 * (4 * C + ALL_E)].rearrange("p (c n) -> p c n", c=2)
        raw_emb = p0_all[1][:].rearrange("p a b -> p (a b)")[:, 0:KIN * C].rearrange("p (k c) -> p k c", k=KIN)
        p1 = [buf(f"p_k1_{i}", [T, HEADS, T]) for i in range(2)]
        tri_raw, pos_sb = (p1[0][:, 4 * i:4 * i + 4, :] for i in range(2))
        pos_sb = pos_sb.rearrange("p a b -> p (a b)")[:, 0:2 * C].rearrange("p (t c) -> p t c", t=2)
        rden = buf("rden", [T, 2, HEADS])
        att = buf("att", [T, 2, C])
        att_t = [buf(f"att_t_{a}", [128, 2, ROWS], F32R) for a in ("hi", "lo")]
        h1 = [buf(f"h1_{i}", [T, 2, C]) for i in range(2)]
        n2 = [buf(f"n2_{i}", [T, 2, C]) for i in range(2)]
        n2t = [buf(f"n2t_{a}", [128, 2, ROWS], F32R) for a in ("hi", "lo")]

        w_raw = [buf(f"w_raw{i}", [128, WC]) for i in range(2)]
        w_part = [buf(f"w_part{i}", [128, 2, WC], F32R) for i in range(2)]

        h_dram = nc.dram_tensor("h_dram", [IMAGES, T, 2, C], F32, kind="Internal").ap()
        qk_dram = [[nc.dram_tensor(f"qk_dram{i}_{a}", [2 * C, ROWS], F32, kind="Internal").ap() for a in range(2)]
                   for i in range(2)]
        max_dram = [nc.dram_tensor(f"max_dram{i}", [HEADS, ROWS], F32, kind="Internal").ap() for i in range(2)]

        s_bank = [psum[:, 0, :], psum[:, 1, :]]
        t_bank = [psum[:, 2, :], psum[:, 3, :]]
        q_bank = [psum[:, 4, :], psum[:, 5, :]]
        o_bank = psum[:, 6, :]
        m_bank = psum[:, 7, :]
        m_half = m_bank[0:CH, 0:2 * ROWS]
        m_rows = m_bank[0:T, 0:2 * C].rearrange("p (t c) -> p t c", t=2)

        wemb_loaded = sem("wemb_loaded")
        const_loaded, const_ready, w_ready = sem("const_loaded"), sem("const_ready"), sem("w_ready")
        minus_set, ones_in = sem("minus_set"), sem("ones_in")
        ms, q_set, pad_set = sem("set_once"), sem("q_set"), sem("pad_set")
        x_loaded = [sem(f"x_loaded{i}") for i in range(2)]
        router_split = sem("router_split")
        xhi_done, xlo_done, emb_split = sem("xhi_done"), sem("xlo_done"), sem("emb_split")
        emb_done = [sem("emb_done0"), sem("emb_done1")]
        emb_sum = [sem("emb_sum0"), sem("emb_sum1")]
        bn = [sem(f"bn_done{i}") for i in range(3)]
        mv_done = [sem(f"mv_done{i}") for i in range(3)]
        ve_done = [sem(f"ve_done{i}") for i in range(3)]
        rs_done = [sem(f"rs_done{i}") for i in range(3)]
        norm1, gamma_done, h_done = sem("norm1"), sem("gamma_done"), sem("h_done")
        h_stored = [sem(f"h_stored{i}") for i in range(2)]
        h_loaded = [sem(f"h_loaded{i}") for i in range(2)]
        n1_done, n1t_done, n1hi_done = sem("n1_done"), sem("n1t_done"), sem("n1hi_done")
        qk_done = [sem("qk_done0"), sem("qk_done1")]
        v_done = sem("v_done")
        rope_mul = [sem("rope_mul0"), sem("rope_mul1")]
        rope_add = [sem("rope_add0"), sem("rope_add1")]
        qt_done = [sem("qt_done0"), sem("qt_done1")]
        qhi_done = [sem("qhi_done0"), sem("qhi_done1")]
        qlo_done = [sem("qlo_done0"), sem("qlo_done1")]
        qk_stored = [sem(f"qk_stored{i}") for i in range(2)]
        stacked = [sem(f"stacked{i}") for i in range(4)]
        s_done, max_done = sem("s_done"), sem("max_done")
        mt_done, max_stored, max_placed = sem("mt_done"), sem("max_stored"), sem("max_placed")
        t_done, exp_done, masked = sem("t_done"), sem("exp_done"), sem("masked")
        pv_done, rden_done, onorm = sem("pv_done"), sem("rden_done"), sem("onorm")
        att_tr, att_hi, proj_done, h1_done_ = sem("att_tr"), sem("att_hi"), sem("proj_done"), sem("h1_done_")
        n2_done, n2t_done, n2hi_done, lg_done = sem("n2_done"), sem("n2t_done"), sem("n2hi_done"), sem("lg_done")
        rows_stored = [sem(f"rows_stored{i}") for i in range(2)]
        chunk_in = [sem(f"chunk_in{i}") for i in range(2)]
        chunk_out = [sem(f"chunk_out{i}") for i in range(2)]
        chunk_hi, chunk_lo = sem("chunk_hi"), sem("chunk_lo")
        misc_read = sem("misc_read")

        def misc_free(pe, at, use):
            k, add = misc_count(at, use)
            wait(pe, misc_read, at, k, add - 1)

        def misc_over(eng, at, use):
            k, add = misc_count(at, use)
            wait(eng, misc_read, at, k, add)

        def wait_dma(eng, sems, at, per, back=0):
            n = len(sems)
            if at.static:
                j = at.n - back
                if j >= 0:
                    eng.wait_ge(sems[j % n], per * (j // n + 1))
                return
            u = (at.u - back) % n
            assert per % n == 0
            reg_wait(eng, sems[u], (at.n - back) * (per // n) + (per - per // n * u))

        with nc.Block() as block:
            @block.sync
            def _(sp):
                def load_x(at):
                    if at is None:
                        return
                    wait(sp, xlo_done, at, 1, 0)
                    sp.dma_start(x_in[:], x[bass.ds(at.n, 1)].rearrange("b p k t -> (b p) k t"))\
                        .then_inc(x_loaded[at.u % 2], 16)

                sp.dma_start(raw_emb, w_emb).then_inc(wemb_loaded, 16)
                load_x(At(0, 0))
                sp.dma_start(first[:], ident[0:1, 0:1]).then_inc(started[0], 16)
                sp.dma_start(identity[:], ident).then_inc(const_loaded, 16)
                for i in range(2):
                    sp.dma_start(w_raw[i][0:1, 0:1], ident[0:1, 0:1]).then_inc(chunk_out[i], 16)
                sp.dma_start(table[:], tok_rows).then_inc(const_loaded, 16)
                sp.dma_start(pos_sb, pos).then_inc(const_loaded, 16)
                sp.dma_start(gamma_sb[:], gamma.partition_broadcast(T)).then_inc(const_loaded, 16)
                sp.dma_start(beta_sb[:], beta.partition_broadcast(T)).then_inc(const_loaded, 16)
                sp.dma_start(br_sb[:], b_router.partition_broadcast(T)).then_inc(const_loaded, 16)
                sp.dma_start(cos_sb[:], cos).then_inc(const_loaded, 16)
                sp.dma_start(sin_sb[:], sin).then_inc(const_loaded, 16)
                sp.dma_start(tri_raw, tri).then_inc(const_loaded, 16)
                sp.dma_start(raw[:, :, QK], w_qk).then_inc(const_loaded, 16)
                sp.dma_start(raw[:, :, VV], w_v).then_inc(const_loaded, 16)
                sp.dma_start(raw[:, :, PJ], w_proj).then_inc(const_loaded, 16)
                sp.dma_start(raw[:, :, RT], w_router).then_inc(const_loaded, 16)


                sp.wait_ge(minus_set, 1)
                for i in range(4):
                    sp.dma_start(k_st[i][MROW:MROW + 1].bitcast(F32), q_st[0][0:1].bitcast(F32)).then_inc(ones_in, 16)

                def store_h(at):
                    if at is None:
                        return
                    wait(sp, h_done, at, 1, 1)
                    sp.dma_start(h_dram[bass.ds(at.n, 1)].rearrange("b p t c -> (b p) t c"), h_new[at.u % 2][:])\
                        .then_inc(h_stored[at.u % 2], 16)

                def load_h(at):
                    if at is None:
                        return
                    wait_dma(sp, h_stored, at, 16)
                    misc_over_back(sp, at, "PROJ", 2)
                    sp.dma_start(h_old[at.u % 2][:], h_dram[bass.ds(at.n, 1)].rearrange("b p t c -> (b p) t c"))\
                        .then_inc(h_loaded[at.u % 2], 16)

                def place_max(at):
                    if at is None:
                        return
                    misc_over(sp, at, "MT")
                    wait(sp, max_placed, at, 16, 0)
                    sp.dma_start(max_dram[at.u % 2], rmax_t[:].bitcast(F32)).then_inc(max_stored, 16)
                    wait(sp, max_stored, at, 16, 16)
                    sp.dma_start(q_st[at.u][MROW:MROW + 1].bitcast(F32), max_dram[at.u % 2].unsqueeze(0))\
                        .then_inc(max_placed, 16)

                def stack(at):
                    if at is None:
                        return
                    for a, done in enumerate((qhi_done, qlo_done)):
                        wait(sp, done[0], at, 1, 1)
                        wait(sp, done[1], at, 1, 1)
                        wait_dma(sp, stacked, at, 96, back=2)
                        sp.dma_start(qk_dram[at.u % 2][a].rearrange("(c p) t -> p c t", p=CH), qkt[a][:].bitcast(F32))\
                            .then_inc(qk_stored[at.u % 2], 16)
                    wait(sp, t_done, at, SLOTS, -3 * SLOTS)
                    if at.static and at.n == 0:
                        sp.wait_ge(ms, 9)
                        sp.wait_ge(q_set, 4)
                    wait_dma(sp, qk_stored, at, 32)
                    for r, (qa, ka) in enumerate(((0, 0), (1, 0), (0, 1))):
                        for st, a, c in ((q_st, qa, 0), (k_st, ka, 1)):
                            sp.dma_start(st[at.u][r * D:(r + 1) * D].bitcast(F32),
                                         qk_dram[at.u % 2][a][c * C:(c + 1) * C].rearrange("(h d) t -> d h t", d=D))\
                                .then_inc(stacked[at.u], 16)

                def store_rows(at):
                    if at is None:
                        return
                    wait(sp, n2_done, at, 1, 1)
                    rows = expert_in.rearrange("(b t p) c -> b p t c", b=IMAGES, t=2)
                    sp.dma_start(rows[bass.ds(at.n, 1), :, :, 0:C].rearrange("b p t c -> (b p) t c"), n2[at.u % 2][:])\
                        .then_inc(rows_stored[at.u % 2], 16)
                    rows = out.rearrange("(b t p) c -> b p t c", b=IMAGES, t=2)
                    sp.dma_start(rows[bass.ds(at.n, 1)].rearrange("b p t c -> (b p) t c"), h1[at.u % 2][:])\
                        .then_inc(rows_stored[at.u % 2], 16)

                def misc_over_back(eng, at, use, back):
                    if at.static:
                        if at.n >= back:
                            misc_over(eng, At(at.n - back, 0), use)
                    else:
                        misc_over(eng, At(at.n - back, 0), use)

                def load_chunk(s):
                    if s.static:
                        return
                    c, p = s.n - LOOP_FROM, s.c % 2
                    reg_wait(sp, chunk_lo, c + 1)
                    if s.c < LOOP_FROM + 2:
                        sp.wait_ge(chunk_out[p], 16)
                    sp.dma_start(w_raw[p][:], w_experts[bass.ds(c, 1)].rearrange("q p n -> (q p) n"))\
                        .then_inc(chunk_in[p], 16)

                def store_chunk(s):
                    if s.static:
                        return
                    c, p = s.n - LOOP_FROM, s.c % 2
                    reg_wait(sp, chunk_lo, c + 3)
                    sp.dma_start(w_parts[bass.ds(c, 1)].rearrange("q p n -> (q p) n"),
                                 w_part[p][:].bitcast(F32).rearrange("p a n -> p (a n)")).then_inc(chunk_out[p], 16)

                def step(s):
                    load_chunk(s)
                    if not (s.static and s.n == 0):
                        load_x(s.image(0))
                    place_max(s.image(4))
                    store_h(s.image(1))
                    load_h(s.image(5))
                    stack(s.image(2))
                    store_rows(s.image(6))
                    store_chunk(s)
                run_steps(sp, step)
                for i in range(2):
                    sp.wait_ge(rows_stored[i], 32 * IMAGES // 2)
                    sp.wait_ge(chunk_out[i], 16 + 16 * (ALL_E * QE // 2))

            @block.tensor
            def _(pe):
                def first_image(at, sem, count):
                    if at.static and at.n == 0:
                        pe.wait_ge(sem, count)

                def embed(at, t):
                    if at is None:
                        return
                    if t == 0:
                        first_image(at, emb_split, 2)
                        wait(pe, xlo_done, at, 1, 1)
                    wait(pe, qlo_done[t], at, 1, -1)
                    for k in range(KIN):
                        mm = split3(pe, q_bank[t][0:T, 0:C], x_hi[:, k, t * T:(t + 1) * T],
                                    x_lo[:, k, t * T:(t + 1) * T], wemb[0][:, k, :], wemb[1][:, k, :],
                                    k == 0, k == KIN - 1)
                    mm.then_inc(emb_done[t], 1)

                def turn(src, done):
                    for t in range(2):
                        for c in range(2):
                            mm = pe.transpose(m_half[:, c * ROWS + t * T:c * ROWS + (t + 1) * T],
                                              src[:, t, c * CH:(c + 1) * CH], identity[0:T, 0:T])
                    mm.then_inc(done, 1)

                def n1_turn(at):
                    if at is None:
                        return
                    misc_free(pe, at, "N1T")
                    first_image(at, const_loaded, 16 * 13)
                    wait(pe, n1_done, at, 1, 1)
                    turn(n1, n1t_done)

                def qk(at, t):
                    if at is None:
                        return
                    if t == 0:
                        first_image(at, w_ready, 6)
                        first_image(at, pad_set, 8)
                        misc_over(pe, at, "N1T")
                    wait(pe, emb_sum[t], at, 1, 2, IMAGES)
                    for c in range(2):
                        mm = split3(pe, q_bank[t][0:T, 0:2 * C], n1t[0][:, c, t * T:(t + 1) * T],
                                    n1t[1][:, c, t * T:(t + 1) * T], whi[:, c, QK], wlo[:, c, QK], c == 0, c == 1)
                    mm.then_inc(qk_done[t], 1)

                def v(at):
                    if at is None:
                        return
                    misc_free(pe, at, "V")
                    for t in range(2):
                        for c in range(2):
                            mm = split3(pe, m_rows[:, t, :], n1t[0][:, c, t * T:(t + 1) * T],
                                        n1t[1][:, c, t * T:(t + 1) * T], whi[:, c, VV], wlo[:, c, VV], c == 0, c == 1)
                    mm.then_inc(v_done, 1)

                def qk_turn(at, b):
                    if at is None:
                        return
                    wait(pe, rope_mul[b], at, 1, 1)
                    for t in range(2):
                        wait(pe, rope_add[t], at, 1, 1)
                    for cc in range(2):
                        for t in range(2):
                            col = (2 * b + cc) * CH
                            mm = pe.transpose(q_bank[b][0:CH, cc * ROWS + t * T:cc * ROWS + (t + 1) * T],
                                              qkr[:, t, col:col + CH], identity[0:T, 0:T])
                    mm.then_inc(qt_done[b], 1)

                def scores(at, g):
                    if at is None:
                        return
                    if g == 0:
                        wait_dma(pe, stacked, at, 96)
                        first_image(at, ms, 9)
                        first_image(at, q_set, 4)
                        first_image(at, ones_in, 64)
                        first_image(at, const_ready, 3)
                    wait(pe, max_done, at, SLOTS, g - 1)
                    bank = s_bank[(at.u + g) % 2]
                    q, k = q_st[at.u], k_st[at.u]
                    if g < 3:
                        pe.matmul(bank[0:T, 0:4 * T], eye16[:], tri_sb[:].rearrange("p a b -> p (a b)"),
                                  start=True, stop=False, skip_group_check=True)
                        for i in range(4):
                            h = 4 * g + i
                            mm = pe.matmul(bank[0:T, i * T:(i + 1) * T], q[0:KP, h, 0:T], k[0:KP, h, 0:T],
                                           start=False, stop=(i == 3), skip_group_check=True)
                    else:
                        two_heads = bank[0:T, 0:2 * ROWS].rearrange("p (h k) -> p h k", h=2)
                        pe.matmul(two_heads[:, :, T:ROWS], eye16[:], tri_sb[:, 0:2, :],
                                  start=True, stop=False, skip_group_check=True)
                        for i in range(2):
                            h = 2 * (g - 3) + i
                            mm = pe.matmul(two_heads[:, i, :], q[0:KP, h, T:ROWS], k[0:KP, h, :],
                                           start=False, stop=(i == 1), skip_group_check=True)
                    mm.then_inc(s_done, 1)

                def max_turn(at):
                    if at is None:
                        return
                    misc_free(pe, at, "MT")
                    wait(pe, max_done, at, SLOTS, SLOTS)
                    for t in range(2):
                        mm = pe.transpose(m_bank[0:HEADS, t * T:(t + 1) * T], rmax[at.u % 2][:, t, :], identity[0:T, 0:T])
                    mm.then_inc(mt_done, 1)

                def scores_t(at, g):
                    if at is None:
                        return
                    if g == 0:
                        wait(pe, max_placed, at, 16, 16)
                    wait(pe, exp_done, at, SLOTS, g - 1)
                    bank = t_bank[(at.u + g) % 2]
                    q, k = q_st[at.u], k_st[at.u]
                    kind, n = T_GROUPS[g]
                    if kind == "k1":
                        for i in range(4):
                            mm = pe.matmul(bank[0:T, i * T:(i + 1) * T], k[:, 4 * n + i, T:ROWS], q[:, 4 * n + i, T:ROWS],
                                           start=True, stop=True)
                    else:
                        for i in range(2):
                            mm = pe.matmul(bank[0:T, i * ROWS:(i + 1) * ROWS], k[:, 2 * n + i, 0:T], q[:, 2 * n + i, :],
                                           start=True, stop=True)
                    mm.then_inc(t_done, 1)

                def pv(at, pair):
                    if at is None:
                        return
                    if pair == 0:
                        wait(pe, onorm, at, 1, 0)
                        misc_over(pe, at, "V")
                    wait(pe, masked, at, SLOTS, PAIR_GROUP[pair] + 1)
                    for h in (2 * pair, 2 * pair + 1):
                        o = [o_bank[0:T, (t * HEADS + h) * (D + 1):(t * HEADS + h + 1) * (D + 1)] for t in range(2)]
                        pr, va = p0[at.u % 2], v_aug[at.u]
                        pe.matmul(o[0], pr[:, h, 0:T], va[:, 0, h, :], start=True, stop=True)
                        pe.matmul(o[1], pr[:, h, T:ROWS], va[:, 0, h, :], start=True, stop=False)
                        mm = pe.matmul(o[1], p1[at.u % 2][:, h, :], va[:, 1, h, :], start=False, stop=True)
                    mm.then_inc(pv_done, 1)

                def att_turn(at):
                    if at is None:
                        return
                    misc_free(pe, at, "ATT")
                    wait(pe, onorm, at, 1, 1)
                    turn(att, att_tr)

                def project(at):
                    if at is None:
                        return
                    misc_free(pe, at, "PROJ")
                    for t in range(2):
                        for c in range(2):
                            mm = split3(pe, m_rows[:, t, :], att_t[0][:, c, t * T:(t + 1) * T],
                                        att_t[1][:, c, t * T:(t + 1) * T], whi[:, c, PJ], wlo[:, c, PJ], c == 0, c == 1)
                    mm.then_inc(proj_done, 1)

                def n2_turn(at):
                    if at is None:
                        return
                    misc_free(pe, at, "N2T")
                    wait(pe, n2_done, at, 1, 1)
                    turn(n2[at.u % 2], n2t_done)

                def router(at):
                    if at is None:
                        return
                    misc_free(pe, at, "LG")
                    for t in range(2):
                        for c in range(2):
                            at16 = t * 2 * ALL_E
                            pe.matmul(m_bank[0:T, at16:at16 + 2 * ALL_E], n2t[0][:, c, t * T:(t + 1) * T],
                                      router_w[:, c, :], start=(c == 0), stop=False, skip_group_check=True)
                            mm = pe.matmul(m_bank[0:T, at16:at16 + ALL_E], n2t[1][:, c, t * T:(t + 1) * T],
                                           router_w[:, c, 0:ALL_E], start=False, stop=(c == 1), skip_group_check=True)
                    mm.then_inc(lg_done, 1)

                def step(s):
                    i = s.image
                    scores(i(4), 7)
                    scores_t(i(5), 2)
                    qk(i(2), 0)
                    scores(i(4), 8)
                    scores_t(i(5), 3)
                    qk(i(2), 1)
                    pv(i(5), 0)
                    att_turn(i(6))
                    scores(i(3), 0)
                    scores_t(i(5), 4)
                    pv(i(5), 1)
                    v(i(2))
                    scores(i(3), 1)
                    scores_t(i(5), 5)
                    max_turn(i(4))
                    scores(i(3), 2)
                    scores_t(i(5), 6)
                    pv(i(5), 2)
                    project(i(6))
                    qk_turn(i(2), 0)
                    scores(i(3), 3)
                    scores_t(i(5), 7)
                    pv(i(5), 3)
                    router(i(7))
                    qk_turn(i(2), 1)
                    scores(i(3), 4)
                    scores_t(i(5), 8)
                    scores(i(3), 5)
                    scores_t(i(4), 0)
                    n1_turn(i(1))
                    embed(i(0), 0)
                    pv(i(5), 4)
                    scores(i(3), 6)
                    scores_t(i(4), 1)
                    n2_turn(i(6))
                    embed(i(0), 1)
                    pv(i(5), 5)
                run_steps(pe, step)

            @block.scalar
            def _(act):
                def patches_hi(at):
                    if at is None:
                        return
                    wait_dma(act, x_loaded, at, 16)
                    wait(act, emb_done[1], at, 1, 0)
                    act.copy(x_hi[:].rearrange("p k t -> p (k t)"),
                             x_in[:].rearrange("p k t -> p (k t)")).then_inc(xhi_done, 1)

                act.wait_ge(wemb_loaded, 16)
                act.copy(wemb[0][:], raw_emb).then_inc(emb_split, 1)
                act.wait_ge(const_loaded, 16 * 13)
                for c in range(2):
                    act.copy(whi[0:CH, c, :], raw[:, c, :]).then_inc(w_ready, 1)

                def n1_hi(at):
                    if at is None:
                        return
                    wait(act, n1t_done, at, 1, 1)
                    wait(act, v_done, at, 1, 0)
                    act.copy(n1t[0][0:CH].rearrange("p a b -> p (a b)"), m_half).then_inc(n1hi_done, 1)

                def values(at):
                    if at is None:
                        return
                    wait(act, v_done, at, 1, 1)
                    if at.static and at.n == 0:
                        act.wait_ge(ms, 9)
                    wait(act, pv_done, at, 6, -18)
                    act.copy(v_aug[at.u][:, :, :, 0:D], m_rows.rearrange("p t (h d) -> p t h d", d=D))\
                        .then_inc(misc_read, 1)

                def qk_hi(at, b):
                    if at is None:
                        return
                    wait(act, qt_done[b], at, 1, 1)
                    wait_dma(act, qk_stored, at, 32, back=1)
                    act.copy(qkt[0][:, 2 * b:2 * b + 2, :].rearrange("p a b -> p (a b)"), q_bank[b][0:CH, 0:2 * ROWS])\
                        .then_inc(qhi_done[b], 1)

                def max_out(at):
                    if at is None:
                        return
                    wait(act, mt_done, at, 1, 1)
                    wait(act, max_stored, at, 16, 0)
                    act.copy(rmax_t[:], m_bank[0:HEADS, 0:ROWS]).then_inc(misc_read, 1)

                def exps(at, g):
                    if at is None:
                        return
                    wait(act, t_done, at, SLOTS, g + 1)
                    wait(act, pv_done, at, 6, -6)
                    kind, n = T_GROUPS[g]
                    bank = t_bank[(at.u + g) % 2][0:T, 0:2 * ROWS]
                    dst = p1[at.u % 2][:, 4 * n:4 * n + 4, :] if kind == "k1" else p0[at.u % 2][:, 2 * n:2 * n + 2, :]
                    act.activation(dst.rearrange("p a b -> p (a b)"), bank, ACT.Exp, scale=float(D) ** -0.5)\
                        .then_inc(exp_done, 1)

                def chunk_hi_part(s):
                    if s.static:
                        return
                    c, p = s.n - LOOP_FROM, s.c % 2
                    reg_wait(act, chunk_in[p], (c - p) * 8 + 16)
                    reg_wait(act, chunk_out[p], (c - p) * 8 + 16)
                    act.copy(w_part[p][:, 0, :], w_raw[p][:]).then_inc(chunk_hi, 1)

                def att_hi_part(at):
                    if at is None:
                        return
                    wait(act, att_tr, at, 1, 1)
                    wait(act, proj_done, at, 1, 0)
                    act.copy(att_t[0][0:CH].rearrange("p a b -> p (a b)"), m_half).then_inc(att_hi, 1)

                def n2_hi(at):
                    if at is None:
                        return
                    wait(act, n2t_done, at, 1, 1)
                    wait(act, lg_done, at, 1, 0)
                    act.copy(n2t[0][0:CH].rearrange("p a b -> p (a b)"), m_half).then_inc(n2hi_done, 1)

                def step(s):
                    i = s.image
                    exps(i(5), 2)
                    exps(i(5), 3)
                    att_hi_part(i(6))
                    exps(i(5), 4)
                    values(i(2))
                    exps(i(5), 5)
                    patches_hi(i(0))
                    chunk_hi_part(s)
                    max_out(i(4))
                    exps(i(5), 6)
                    qk_hi(i(2), 0)
                    exps(i(5), 7)
                    qk_hi(i(2), 1)
                    exps(i(5), 8)
                    exps(i(4), 0)
                    n1_hi(i(1))
                    exps(i(4), 1)
                    n2_hi(i(6))
                run_steps(act, step)

            @block.vector
            def _(dve):
                def patches_lo(at):
                    if at is None:
                        return
                    wait(dve, xhi_done, at, 1, 1)
                    dve.tensor_tensor(x_lo[:].rearrange("p k t -> p (k t)"), x_in[:].rearrange("p k t -> p (k t)"),
                                      x_hi[:].bitcast(F32).rearrange("p k t -> p (k t)"), ALU.subtract)\
                        .then_inc(xlo_done, 1)

                dve.wait_ge(emb_split, 1)
                dve.tensor_tensor(wemb[1][:], raw_emb, wemb[0][:].bitcast(F32), ALU.subtract)\
                    .then_inc(emb_split, 1)
                dve.wait_ge(const_loaded, 16 * 13)
                dve.tensor_tensor(table[:], table[:], pos_sb, ALU.add).then_inc(const_ready, 1)
                dve.tensor_copy(eye16[:], identity[0:T, 0:T]).then_inc(const_ready, 1)
                dve.tensor_copy(tri_sb[:], tri_raw).then_inc(const_ready, 1)
                for i in range(2):
                    dve.memset(w_part[i][0:1, 1, 0:1].bitcast(F32), 0.0).then_inc(chunk_lo, 1)
                dve.wait_ge(ones_in, 64)
                for i in range(4):
                    dve.memset(q_st[i][0:KP].bitcast(F32), 0.0).then_inc(q_set, 1)
                dve.wait_ge(w_ready, 2)
                for c in range(2):
                    dve.tensor_tensor(wlo[0:CH, c, :], raw[:, c, :], whi[0:CH, c, :].bitcast(F32), ALU.subtract)\
                        .then_inc(w_ready, 1)
                for a, w in enumerate((whi, wlo, *n1t, *att_t, *n2t)):
                    dve.memset(w[CH:128].bitcast(F32), 0.0).then_inc(pad_set, 1)
                dve.wait_ge(pad_set, 8)
                dve.wait_ge(w_ready, 4)
                for a, w in enumerate((whi, wlo)):
                    dve.tensor_copy(router_w[:, :, a * ALL_E:(a + 1) * ALL_E], w[:, :, RT].bitcast(F32))\
                        .then_inc(w_ready, 1)
                dve.wait_ge(const_ready, 3)

                def sum_rows(at, t):
                    if at is None:
                        return
                    wait(dve, emb_done[t], at, 1, 1)
                    dve.tensor_tensor(xs[:, t, :], q_bank[t][0:T, 0:C], table[:, t, :], ALU.add).then_inc(emb_sum[t], 1)

                def stats(at, n, src):
                    for t in range(2):
                        ins = dve.bn_stats(stat[n][:, t, :], src[:, t, :])
                    ins.then_inc(bn[n], 1)
                    wait(dve, bn[n], at, 1, 1, alone=True)
                    for t in range(2):
                        ins = dve.bn_aggr(mv[n][:, t, :], stat[n][:, t, :])
                    ins.then_inc(mv_done[n], 1)

                def norm(at, n, src, dst, done):
                    wait(dve, rs_done[n], at, 1, 1)
                    for t in range(2):
                        ins = dve.tensor_scalar(dst[:, t, :], src[:, t, :], mv[n][:, t, 0:1], rstd[n][:, t:t + 1],
                                                ALU.subtract, ALU.mult)
                    ins.then_inc(done, 1)

                def stats1(at):
                    if at is None:
                        return
                    wait(dve, emb_sum[1], at, 1, 1)
                    stats(at, 0, xs)

                def norm1_rows(at):
                    if at is None:
                        return
                    wait(dve, h_done, at, 1, 0)
                    norm(at, 0, xs, xn, norm1)

                def stats2(at):
                    if at is None:
                        return
                    wait(dve, h_done, at, 1, 1)
                    stats(at, 1, h_new[at.u % 2])

                def norm2_rows(at):
                    if at is None:
                        return
                    wait(dve, n1t_done, at, 1, 0)
                    norm(at, 1, h_new[at.u % 2], n1, n1_done)

                def n1_lo(at):
                    if at is None:
                        return
                    wait(dve, n1hi_done, at, 1, 1)
                    dve.tensor_tensor(n1t[1][0:CH].rearrange("p a b -> p (a b)"), m_half,
                                      n1t[0][0:CH].bitcast(F32).rearrange("p a b -> p (a b)"), ALU.subtract)\
                        .then_inc(misc_read, 1)

                def rope(at, t):
                    if at is None:
                        return
                    wait(dve, qk_done[t], at, 1, 1)
                    wait(dve, rope_add[t], at, 1, 0)
                    heads = 2 * HEADS
                    src = q_bank[t][0:T, 0:2 * C].rearrange("p (h d) -> p h d", d=D)
                    dc = roped[t][:].rearrange("p (h d) -> p h d", d=D)
                    ds = ropes[t][:].rearrange("p (h d) -> p h d", d=D)
                    cosb = cos_sb[:, t, :].unsqueeze(1).to_broadcast([T, heads, D])
                    dve.tensor_tensor(dc, src, cosb, ALU.mult)
                    for a in range(2):
                        to, fr = slice(a * D // 2, (a + 1) * D // 2), slice((1 - a) * D // 2, (2 - a) * D // 2)
                        ins = dve.tensor_tensor(ds[:, :, to], src[:, :, fr],
                                                sin_sb[:, t, to].unsqueeze(1).to_broadcast([T, heads, D // 2]), ALU.mult)
                    ins.then_inc(rope_mul[t], 1)

                def qk_lo(at, b):
                    if at is None:
                        return
                    wait(dve, qhi_done[b], at, 1, 1)
                    wait_dma(dve, qk_stored, at, 32, back=1)
                    dve.tensor_tensor(qkt[1][:, 2 * b:2 * b + 2, :].rearrange("p a b -> p (a b)"),
                                      q_bank[b][0:CH, 0:2 * ROWS],
                                      qkt[0][:, 2 * b:2 * b + 2, :].bitcast(F32).rearrange("p a b -> p (a b)"),
                                      ALU.subtract).then_inc(qlo_done[b], 1)

                def row_max(at, g):
                    if at is None:
                        return
                    wait(dve, s_done, at, SLOTS, g + 1)
                    if g == 0:
                        wait(dve, mt_done, at, 1, -1)
                    bank = s_bank[(at.u + g) % 2][0:T, 0:2 * ROWS]
                    if g < 3:
                        dve.tensor_reduce(rmax[at.u % 2][:, 0, 4 * g:4 * g + 4], bank.rearrange("p (h k) -> p h k", h=4),
                                          AX.X, ALU.max).then_inc(max_done, 1)
                    else:
                        dve.tensor_reduce(rmax[at.u % 2][:, 1, 2 * (g - 3):2 * (g - 3) + 2],
                                          bank.rearrange("p (h k) -> p h k", h=2), AX.X, ALU.max).then_inc(max_done, 1)

                def normalise(at):
                    if at is None:
                        return
                    wait(dve, pv_done, at, 6, 6)
                    o = o_bank[0:T, 0:2 * HEADS * (D + 1)].rearrange("p (h d) -> p h d", d=D + 1)
                    dve.reciprocal(rden[:].rearrange("p t h -> p (t h)"), o[:, :, D]).then_inc(rden_done, 1)
                    wait(dve, rden_done, at, 1, 1)
                    wait(dve, att_tr, at, 1, 0)
                    dve.tensor_tensor(att[:].rearrange("p t (h d) -> p (t h) d", d=D), o[:, :, 0:D],
                                      rden[:].rearrange("p t h -> p (t h)").unsqueeze(2)
                                      .to_broadcast([T, 2 * HEADS, D]), ALU.mult).then_inc(onorm, 1)

                def att_lo(at):
                    if at is None:
                        return
                    wait(dve, att_hi, at, 1, 1)
                    dve.tensor_tensor(att_t[1][0:CH].rearrange("p a b -> p (a b)"), m_half,
                                      att_t[0][0:CH].bitcast(F32).rearrange("p a b -> p (a b)"), ALU.subtract)\
                        .then_inc(misc_read, 1)

                def residual(at):
                    if at is None:
                        return
                    wait(dve, proj_done, at, 1, 1)
                    wait_dma(dve, h_loaded, at, 16)
                    wait_dma(dve, rows_stored, at, 32, back=2)
                    dve.tensor_tensor(h1[at.u % 2][:], m_rows, h_old[at.u % 2][:], ALU.add).then_inc(misc_read, 1)
                    misc_over(dve, at, "PROJ")
                    stats(at, 2, h1[at.u % 2])

                def norm3_rows(at):
                    if at is None:
                        return
                    wait(dve, n2t_done, at, 1, -1)
                    norm(at, 2, h1[at.u % 2], n2[at.u % 2], n2_done)

                def n2_lo(at):
                    if at is None:
                        return
                    wait(dve, n2hi_done, at, 1, 1)
                    dve.tensor_tensor(n2t[1][0:CH].rearrange("p a b -> p (a b)"), m_half,
                                      n2t[0][0:CH].bitcast(F32).rearrange("p a b -> p (a b)"), ALU.subtract)\
                        .then_inc(misc_read, 1)

                def chunk_lo_part(s):
                    if s.static:
                        return
                    c, p = s.n - LOOP_FROM, s.c % 2
                    reg_wait(dve, chunk_hi, c + 1)
                    dve.tensor_tensor(w_part[p][:, 1, :], w_raw[p][:], w_part[p][:, 0, :].bitcast(F32), ALU.subtract)\
                        .then_inc(chunk_lo, 1)

                def add_router_bias(at):
                    if at is None:
                        return
                    wait(dve, lg_done, at, 1, 1)
                    both = m_bank[0:T, 0:4 * ALL_E].rearrange("p (t a e) -> p t a e", t=2, a=2)
                    dve.tensor_tensor(logits_lo[:], both[:, :, 1, :], br_sb[:].unsqueeze(1).to_broadcast([T, 2, ALL_E]),
                                      ALU.add).then_inc(router_split, 1)
                    wait(dve, router_split, at, 1, 1)
                    dve.tensor_tensor(logits[:, bass.ds(at.n * 2, 2), :], both[:, :, 0, :], logits_lo[:], ALU.add)\
                        .then_inc(misc_read, 1)

                def step(s):
                    i = s.image
                    sum_rows(s.image(1), 1)
                    row_max(i(4), 7)
                    normalise(i(6))
                    rope(i(2), 0)
                    stats1(i(1))
                    row_max(i(4), 8)
                    norm1_rows(i(1))
                    att_lo(i(6))
                    rope(i(2), 1)
                    row_max(i(3), 0)
                    row_max(i(3), 1)
                    stats2(i(1))
                    row_max(i(3), 2)
                    patches_lo(i(0))
                    norm2_rows(i(1))
                    residual(i(6))
                    qk_lo(i(2), 0)
                    row_max(i(3), 3)
                    add_router_bias(i(7))
                    qk_lo(i(2), 1)
                    row_max(i(3), 4)
                    norm3_rows(i(6))
                    chunk_lo_part(s)
                    row_max(i(3), 5)
                    n1_lo(i(1))
                    row_max(i(3), 6)
                    n2_lo(i(6))
                    sum_rows(i(0), 0)
                run_steps(dve, step)

            @block.gpsimd
            def _(pool):
                pool.memset(q_st[0][0:1].bitcast(F32), -1.0).then_inc(minus_set, 1)
                pool.wait_ge(minus_set, 1)
                for i in range(4):
                    if i >= 1:
                        pool.wait_ge(ms, 2 * i)
                    pool.memset(v_aug[i][:], 1.0).then_inc(ms, 1)
                    pool.wait_ge(ms, 2 * i + 1)
                    pool.memset(k_st[i][0:KP].bitcast(F32), 0.0).then_inc(ms, 1)
                pool.wait_ge(ms, 8)
                pool.memset(half[:], -0.5).then_inc(ms, 1)
                pool.wait_ge(ms, 9)

                def root(at, n):
                    wait(pool, mv_done[n], at, 1, 1, alone=True)
                    pool.tensor_scalar(var_eps[n][:], mv[n][:, :, 1], EPS, None, ALU.add).then_inc(ve_done[n], 1)
                    wait(pool, ve_done[n], at, 1, 1)
                    pool.tensor_tensor(rstd[n][:], var_eps[n][:], half[:], ALU.pow).then_inc(rs_done[n], 1)

                def root_of(at, n):
                    if at is not None:
                        root(at, n)

                def affine(at):
                    if at is None:
                        return
                    wait(pool, norm1, at, 1, 1)
                    g = gamma_sb[:].unsqueeze(1).to_broadcast([T, 2, C])
                    b = beta_sb[:].unsqueeze(1).to_broadcast([T, 2, C])
                    pool.tensor_tensor(xn[:], xn[:], g, ALU.mult).then_inc(gamma_done, 1)
                    wait(pool, gamma_done, at, 1, 1)
                    wait(pool, n1_done, at, 1, -1)
                    wait_dma(pool, h_stored, at, 16, back=2)
                    pool.tensor_tensor(h_new[at.u % 2][:], xn[:], b, ALU.add).then_inc(h_done, 1)

                def rope_sum(at, t):
                    if at is None:
                        return
                    wait(pool, rope_mul[t], at, 1, 1)
                    wait(pool, qt_done[1], at, 1, 0)
                    pool.tensor_tensor(qkr[:, t, :], roped[t][:], ropes[t][:], ALU.add).then_inc(rope_add[t], 1)

                def causal(at, g):
                    if at is None:
                        return
                    wait(pool, exp_done, at, SLOTS, g + 1, alone=True)
                    kind, n = T_GROUPS[g]
                    d = p1[at.u % 2][:, 4 * n:4 * n + 4, :] if kind == "k1" else p0[at.u % 2][:, 2 * n:2 * n + 2, 0:T]
                    pool.affine_select(out=d, in_=d, compare_op=ALU.is_ge, fill=0.0, base=0,
                                       pattern=[[0, 4 if kind == "k1" else 2], [1, T]], channel_multiplier=-1)\
                        .then_inc(masked, 1)

                def step(s):
                    i = s.image
                    causal(i(5), 2)
                    root_of(i(1), 0)
                    causal(i(5), 3)
                    rope_sum(i(2), 0)
                    affine(i(1))
                    causal(i(5), 4)
                    rope_sum(i(2), 1)
                    causal(i(5), 5)
                    root_of(i(1), 1)
                    causal(i(5), 6)
                    causal(i(5), 7)
                    root_of(i(6), 2)
                    causal(i(5), 8)
                    causal(i(4), 0)
                    causal(i(4), 1)
                run_steps(pool, step)
        clear(nc, used)


def clear(nc, used):
    with nc.Block() as block:
        @block.sync
        def _(sp):
            for s in used:
                sp.sem_clear(s)


def route(nc, sb, sem, psum, logits, lower, valid, lists, expert_in, scale_tiles, tables, place_id):
    with ExitStack() as own:
        def buf(name, shape, dt=F32):
            return sb("r_" + name, shape, dt, own)

        G = SETS * NT
        top, total, pmax, other = (buf(n, [T, NT, SETS]) for n in ("top", "total", "pmax", "other"))
        prob, hot, wgt = (buf(n, [T, NT, ALL_E]) for n in ("prob", "hot", "wgt"))
        order = buf("order", [T, EXPERTS])
        base = buf("base", [T, EXPERTS])
        valid_sb = buf("valid", [T, 2])
        lower_raw = buf("lower_raw", [T, T])
        lower_sb = buf("lower", [T, T], BF16)
        ones16 = buf("ones16", [T, T], BF16)
        ones = buf("ones", [T, NT])
        mask16 = buf("mask16", [T, NT, EXPERTS], BF16)
        tot = buf("tot", [T, EXPERTS, NT])
        incl = buf("incl", [T, EXPERTS, NT])
        pre = buf("pre", [T, NT, EXPERTS])
        work = buf("work", [T, NT, EXPERTS])
        keys = buf("keys", [T, NT, EXPERTS])
        above = buf("above", [T, NT, EXPERTS])
        dropped = buf("dropped", [T, NT])
        place = buf("place", [T, NT])
        pos_u32 = [buf("pos_common", [T, NT], U32), buf("pos_unique", [T, NT], U32)]
        ids = buf("ids", [T, NT], U32)
        cnt = buf("cnt", [T, EXPERTS])
        cnt16 = buf("cnt16", [T, EXPERTS], BF16)
        room = buf("room", [T, EXPERTS])
        thr, cand, gain = buf("thr", [T, EXPERTS]), buf("cand", [T, EXPERTS]), buf("gain", [T, EXPERTS])
        stepv = buf("stepv", [T, 1])
        number = buf("number", [T, ALL_E])
        empty = buf("empty", [128, LIST // 128], U32)
        num_i, tiles_i = buf("num_i", [1, EXPERTS], I32), buf("tiles_i", [1, EXPERTS], I32)
        tiles_f, cum, jump = buf("tiles_f", [1, EXPERTS]), buf("cum", [1, EXPERTS]), buf("jump", [1, EXPERTS])
        slot_i = buf("slot_i", [1, TABLE], I32)
        slot_f, row_f, exp_f, ge_f, flag_f = (buf(n, [1, TABLE]) for n in ("slot_f", "row_f", "exp_f", "ge_f", "flag_f"))

        chain, const_in, pool_set, ids_done = sem("r_chain"), sem("r_const_in"), sem("r_pool_set"), sem("r_ids")
        exp_in, exp_out, mask_ready, prefix_done = sem("r_exp_in"), sem("r_exp_out"), sem("r_mask"), sem("r_prefix")
        cnt_ready, cnt_summed = sem("r_cnt"), sem("r_cnt_sum")
        b_cmp, b_cnt, b_mm, b_gain, b_thr, b_cand = (sem(f"r_b{n}") for n in ("cmp", "cnt", "mm", "gain", "thr", "cand"))
        pos_ready, lists_set, scattered, scales_out = sem("r_pos"), sem("r_lists_set"), sem("r_scat"), sem("r_scales")
        places_out, folded = sem("r_places_out"), sem("r_folded")
        places_in = [sem(f"r_places_in{i}") for i in range(SETS + 1)]
        places = nc.dram_tensor("places", [SETS + 1, T * NT], U32, kind="Internal").ap()
        fold = [buf(f"fold{i}", [128, SCATTERS], U32) for i in range(SETS + 1)]

        POOL_SET = 5 + 2 * EXPERTS
        flat = "p t e -> p (t e)"
        bank_pre = psum[0:T, 0, :]
        bank_tot = psum[0:T, 1, :]
        bank_cnt = psum[0:T, 2, 0:EXPERTS]

        with nc.Block() as block:
            def fold_rows(sp, n, src):
                sp.dma_start(places[n:n + 1].rearrange("o (p t) -> (o p) t", t=NT), src).then_inc(places_out, 16)
                sp.wait_ge(places_out, 16 * {SETS: 1, 0: 2, 1: 3}[n])
                sp.dma_start(fold[n][:], places[n:n + 1].rearrange("o (q j) -> (o q) j", j=SCATTERS))\
                    .then_inc(places_in[n], 16)

            @block.sync
            def _(sp):
                sp.dma_start(valid_sb[:], valid).then_inc(const_in, 16)
                sp.dma_start(lower_raw[:], lower).then_inc(const_in, 16)
                sp.wait_ge(pool_set, 4 + 2 * EXPERTS)
                for n in range(SETS):
                    sp.dma_start(lists[n].rearrange("(p n) o -> p (n o)", p=128), empty[:]).then_inc(lists_set, 16)
                fold_rows(sp, SETS, ids[:])
                sp.wait_ge(pos_ready, 1)
                fold_rows(sp, 0, pos_u32[0][:])
                sp.wait_ge(scales_out, 1)
                sp.dma_start(expert_in.rearrange("(t p) c -> p t c", p=T)[:, :, C:SROW], scale_tiles[:])\
                    .then_inc(const_in, 16)
                sp.wait_ge(pos_ready, 2)
                fold_rows(sp, 1, pos_u32[1][:])
                sp.wait_ge(const_in, 48)

            @block.scalar
            def _(act):
                act.wait_ge(exp_in, 1)
                act.activation(prob[:], logits[:], ACT.Exp).then_inc(exp_out, 1)

            @block.gpsimd
            def _(pool):
                pool.memset(empty[:], EMPTY).then_inc(pool_set, 1)
                for e in range(EXPERTS):
                    pool.memset(order[:, e:e + 1], float(EXPERTS - e)).then_inc(pool_set, 1)
                    pool.memset(base[:, e:e + 1], float(e * REGION)).then_inc(pool_set, 1)
                pool.memset(ones16[:], 1.0).then_inc(pool_set, 1)
                pool.memset(ones[:], 1.0).then_inc(pool_set, 1)
                pool.iota(ids[:], pattern=[[T, NT]], base=0, channel_multiplier=1).then_inc(pool_set, 1)
                pool.iota(slot_i[:], pattern=[[1, TABLE]], base=0, channel_multiplier=0).then_inc(pool_set, 1)
                pool.wait_ge(pool_set, POOL_SET)

                pool.wait_ge(places_in[SETS], 16)
                for n in range(SETS):
                    pool.tensor_copy(place_id[n][:, 0:SCATTERS, 1], fold[SETS][:])
                pool.wait_ge(places_in[0], 16)
                pool.tensor_copy(place_id[0][:, 0:SCATTERS, 0], fold[0][:]).then_inc(folded, 1)
                pool.wait_ge(folded, 1)
                pool.wait_ge(lists_set, 32)
                for t in range(SCATTERS):
                    pool.indirect_dma_start(lists[0],
                                            bass.IndirectOffsetOnAxis(ap=place_id[0][:, t, 0:1], axis=0),
                                            place_id[0][:, t, 1:2], None, bounds_check=LIST - 1, oob_is_err=False)\
                        .then_inc(scattered, 16)
                pool.wait_ge(places_in[1], 16)
                pool.tensor_copy(place_id[1][:, 0:SCATTERS, 0], fold[1][:]).then_inc(folded, 1)
                pool.wait_ge(folded, 2)
                pool.wait_ge(scattered, 16 * SCATTERS)

            @block.tensor
            def _(pe):
                pe.wait_ge(pool_set, POOL_SET)

                def prefix(n):
                    pe.wait_ge(mask_ready, n + 1)
                    m = mask16[:].rearrange(flat)
                    pe.matmul(bank_pre, lower_sb[:], m, start=True, stop=True)
                    pe.matmul(bank_tot, ones16[:], m, start=True, stop=True).then_inc(prefix_done, 1)

                prefix(0)
                with pe.Fori(0, BISECT) as i:
                    pe.wait_ge(b_cnt, i + 1)
                    pe.matmul(bank_cnt, ones16[:], cnt16[:], start=True, stop=True).then_inc(b_mm, 1)
                pe.wait_ge(cnt_ready, 1)
                pe.matmul(bank_cnt, ones16[:], cnt16[:], start=True, stop=True).then_inc(cnt_summed, 1)
                prefix(1)
                prefix(2)

            @block.vector
            def _(dve):
                links = [0]

                def link(ins):
                    links[0] += 1
                    ins.then_inc(chain, 1)
                    dve.wait_ge(chain, links[0])

                def four(ap):
                    return ap.rearrange("p t (s e) -> p (t s) e", s=SETS)

                def pairs(ap):
                    return ap[:].rearrange("p t s -> p (t s)")

                def over(ap):
                    return pairs(ap).unsqueeze(2).to_broadcast([T, G, EXPERTS])

                dve.wait_ge(pool_set, POOL_SET)
                dve.wait_ge(const_in, 32)
                dve.tensor_copy(lower_sb[:], lower_raw[:])
                link(dve.tensor_reduce(pairs(top), four(logits[:]), AX.X, ALU.max))
                dve.tensor_tensor(four(logits[:]), four(logits[:]), over(top), ALU.subtract).then_inc(exp_in, 1)
                dve.wait_ge(exp_out, 1)
                link(dve.tensor_reduce(pairs(total), four(prob[:]), AX.X, ALU.add))
                link(dve.reciprocal(pairs(total), pairs(total)))
                link(dve.tensor_tensor(four(prob[:]), four(prob[:]), over(total), ALU.mult))
                link(dve.tensor_reduce(pairs(pmax), four(prob[:]), AX.X, ALU.max))
                link(dve.reciprocal(pairs(other), pairs(pmax)))
                dve.tensor_tensor(scale_tiles[:], pmax[:], other[:], ALU.mult).then_inc(scales_out, 1)
                link(dve.tensor_tensor(four(wgt[:]), four(prob[:]), over(pmax), ALU.is_equal))
                link(dve.tensor_tensor(four(wgt[:]), four(wgt[:]), order[:].unsqueeze(1).to_broadcast([T, G, EXPERTS]),
                                       ALU.mult))
                link(dve.tensor_reduce(pairs(top), four(wgt[:]), AX.X, ALU.max))
                link(dve.tensor_tensor(four(hot[:]), four(wgt[:]), over(top), ALU.is_equal))
                ok = valid_sb[:].unsqueeze(1).to_broadcast([T, IMAGES, 2])
                for e in range(ALL_E):
                    h = hot[:, :, e].rearrange("p (b t) -> p b t", t=2)
                    ins = dve.tensor_tensor(h, h, ok, ALU.mult)
                link(ins)
                hot_c, hot_u = hot[:, :, 0:EXPERTS], hot[:, :, EXPERTS:ALL_E]

                def ranks(n, mask):
                    dve.tensor_copy(mask16[:], mask).then_inc(mask_ready, 1)
                    dve.wait_ge(prefix_done, n + 1)
                    link(dve.tensor_copy(tot[:], bank_tot.rearrange("p (t e) -> p e t", e=EXPERTS)))
                    for e in range(EXPERTS):
                        ins = dve.tensor_tensor_scan(incl[:, e, :], ones[:], tot[:, e, :], 0.0, ALU.mult, ALU.add)
                    link(ins)
                    link(dve.tensor_tensor(tot[:], incl[:], tot[:], ALU.subtract))
                    link(dve.tensor_tensor(pre[:], bank_pre.rearrange("p (t e) -> p t e", e=EXPERTS),
                                           tot[:].rearrange("p e t -> p t e"), ALU.add))

                def positions(n, mask, member):
                    link(dve.tensor_copy(number[:, n * EXPERTS:(n + 1) * EXPERTS], incl[:, :, NT - 1]))
                    b = base[:].unsqueeze(1).to_broadcast([T, NT, EXPERTS])
                    link(dve.tensor_tensor(work[:], pre[:], b, ALU.add))
                    link(dve.tensor_tensor(work[:], work[:], mask, ALU.mult))
                    link(dve.tensor_reduce(place[:], work[:], AX.X, ALU.add))
                    link(dve.tensor_scalar(work[:, :, 0], member, -float(EMPTY), float(EMPTY), ALU.mult, ALU.add))
                    dve.tensor_tensor(pos_u32[n][:], place[:], work[:, :, 0], ALU.add).then_inc(pos_ready, 1)

                def tile_table(n, table):
                    mine = number[0:1, n * EXPERTS:(n + 1) * EXPERTS]
                    link(dve.tensor_scalar(num_i[:], mine, float(TS - 1), None, ALU.add))
                    link(dve.tensor_scalar(tiles_i[:], num_i[:], TS.bit_length() - 1, None, ALU.arith_shift_right))
                    link(dve.tensor_copy(tiles_f[:], tiles_i[:]))
                    link(dve.tensor_tensor_scan(cum[:], ones[0:1, 0:EXPERTS], tiles_f[:], 0.0, ALU.mult, ALU.add))
                    link(dve.tensor_scalar(jump[:], tiles_f[:], -float(TS), float(REGION), ALU.mult, ALU.add))
                    link(dve.tensor_copy(slot_f[:], slot_i[:]))
                    link(dve.tensor_scalar(row_f[:], slot_f[:], float(TS), None, ALU.mult))
                    link(dve.memset(exp_f[:], float(n * EXPERTS)))
                    for e in range(EXPERTS - 1):
                        link(dve.tensor_scalar(ge_f[:], slot_f[:], cum[:, e:e + 1], None, ALU.is_ge))
                        link(dve.tensor_tensor(exp_f[:], exp_f[:], ge_f[:], ALU.add))
                        link(dve.tensor_scalar(ge_f[:], ge_f[:], jump[:, e:e + 1], None, ALU.mult))
                        link(dve.tensor_tensor(row_f[:], row_f[:], ge_f[:], ALU.add))
                    total = cum[:, EXPERTS - 1:EXPERTS]
                    link(dve.tensor_scalar(ge_f[:], slot_f[:], total, None, ALU.is_ge))
                    link(dve.tensor_scalar(flag_f[:], row_f[:], -1.0, float(NULL_AT), ALU.mult, ALU.add))
                    link(dve.tensor_tensor(flag_f[:], flag_f[:], ge_f[:], ALU.mult))
                    link(dve.tensor_tensor(row_f[:], row_f[:], flag_f[:], ALU.add))
                    link(dve.tensor_copy(table[:, 0:TABLE], row_f[:]))
                    link(dve.tensor_copy(table[:, TABLE:2 * TABLE], exp_f[:]))
                    link(dve.memset(flag_f[:], 1.0))
                    link(dve.tensor_tensor(flag_f[:, 2:TABLE], exp_f[:, 2:TABLE], exp_f[:, 0:TABLE - 2], ALU.not_equal))
                    link(dve.tensor_copy(table[:, 2 * TABLE:3 * TABLE], flag_f[:]))
                    link(dve.tensor_copy(table[:, 3 * TABLE:3 * TABLE + 1], total))
                    link(dve.tensor_scalar(num_i[:, 0:1], total, 3.0, None, ALU.add))
                    link(dve.tensor_scalar(table[:, 3 * TABLE + 1:3 * TABLE + 2], num_i[:, 0:1], 1, None,
                                           ALU.arith_shift_right))

                ranks(0, hot_c)
                link(dve.tensor_reduce(dropped[:], hot_c, AX.X, ALU.add))
                positions(0, hot_c, dropped[:])

                link(dve.memset(thr[:], 0.0))
                pm = pmax[:, :, 0].unsqueeze(2).to_broadcast([T, NT, EXPERTS])
                dve.wait_ge(pos_ready, 1)
                link(dve.tensor_scalar(work[:], hot_c, 1.0, None, ALU.subtract))
                link(dve.tensor_tensor(keys[:], hot_c, pm, ALU.mult))
                link(dve.tensor_tensor(keys[:], keys[:], work[:], ALU.add))
                link(dve.memset(stepv[:], 0.5))
                dve.memset(cand[:], 0.5).then_inc(b_cand, 1)
                with dve.Fori(0, BISECT) as i:
                    dve.wait_ge(b_cand, i + 1)
                    dve.tensor_tensor(above[:], keys[:], cand[:].unsqueeze(1).to_broadcast([T, NT, EXPERTS]), ALU.is_ge)\
                        .then_inc(b_cmp, 1)
                    dve.wait_ge(b_cmp, i + 1)
                    with nc.allow_low_precision("a count up to 128 is exact in bfloat16"):
                        dve.tensor_reduce(cnt16[:], above[:].rearrange("p t e -> p e t"), AX.X, ALU.add)\
                            .then_inc(b_cnt, 1)
                    dve.wait_ge(b_mm, i + 1)
                    dve.tensor_scalar(gain[:], bank_cnt, float(CAPACITY), stepv[:, 0:1], ALU.is_ge, ALU.mult)\
                        .then_inc(b_gain, 1)
                    dve.wait_ge(b_gain, i + 1)
                    dve.tensor_tensor(thr[:], thr[:], gain[:], ALU.add)
                    dve.tensor_scalar(stepv[:], stepv[:], 0.5, None, ALU.mult).then_inc(b_thr, 1)
                    dve.wait_ge(b_thr, i + 1)
                    dve.tensor_scalar(cand[:], thr[:], stepv[:, 0:1], None, ALU.add).then_inc(b_cand, 1)

                t4 = thr[:].unsqueeze(1).to_broadcast([T, NT, EXPERTS])
                link(dve.tensor_tensor(above[:], keys[:], t4, ALU.is_gt))
                with nc.allow_low_precision("a count up to 128 is exact in bfloat16"):
                    dve.tensor_reduce(cnt16[:], above[:].rearrange("p t e -> p e t"), AX.X, ALU.add).then_inc(cnt_ready, 1)
                dve.wait_ge(cnt_summed, 1)
                link(dve.tensor_scalar(room[:], bank_cnt, -1.0, float(CAPACITY), ALU.mult, ALU.add))
                link(dve.tensor_tensor(keys[:], keys[:], t4, ALU.is_equal))
                ranks(1, keys[:])
                link(dve.tensor_tensor(work[:], pre[:], room[:].unsqueeze(1).to_broadcast([T, NT, EXPERTS]), ALU.is_lt))
                link(dve.tensor_tensor(work[:], work[:], keys[:], ALU.mult))
                link(dve.tensor_tensor(work[:], work[:], above[:], ALU.add))
                link(dve.tensor_tensor(work[:], hot_c, work[:], ALU.subtract))
                link(dve.tensor_reduce(dropped[:], work[:], AX.X, ALU.max))
                link(dve.tensor_tensor(hot_u, hot_u, dropped[:].unsqueeze(2).to_broadcast([T, NT, EXPERTS]), ALU.mult))
                ranks(2, hot_u)
                positions(1, hot_u, dropped[:])

                for n in range(SETS):
                    tile_table(n, tables[:, n * COLUMNS:(n + 1) * COLUMNS])


class Tile:

    def __init__(self, w, p):
        self.w, self.p = w, p
        self.static = isinstance(w, int)
        self.n = w * 2 + p


def experts(nc, sb, sem, psum, which, identity, tables, all_lists, place_id, expert_in, w_parts, b1, b2, out):
    LAGS = 4
    PAIRS = TABLE // 2
    table = tables[:, which * COLUMNS:(which + 1) * COLUMNS]
    lists = all_lists[which]
    count_sem = sem

    def sem(name):
        return count_sem(f"{name}_{which}")

    with ExitStack() as own:
        def two(name, shape, dt=F32):
            return [sb(f"e{which}_{name}{i}", shape, dt, own) for i in range(2)]

        w1b, w2b = two("w1", [CH, Q1, 2, WC], F32R), two("w2", [128, Q2, 2, WC], F32R)
        b1b, b2b = two("b1", [128, FT]), two("b2", [128, C])
        idx_in, idx_out = two("idx_in", [128, 2], U32), two("idx_out", [128, 2], U32)
        rows = two("rows", [128, 2, SROW])
        scale = two("scale", [128, 2])
        xt = [two("xt_hi", [CH, 2, TS], F32R), two("xt_lo", [CH, 2, TS], F32R)]
        act_f = two("act", [128, FT, TS])
        act_p = [two("act_hi", [128, FT, TS], F32R), two("act_lo", [128, FT, TS], F32R)]
        ysum = sb(f"e{which}_ysum", [128, 2, C], F32, own)
        placing = two("placing", [128, 2, 2], U32)
        placing_set, placed = sem("e_placing_set"), [sem("e_placed0"), sem("e_placed1")]
        y = two("y", [128, 2, C])

        def twos(name):
            return [sem(f"e_{name}{i}") for i in range(2)]

        rows_set = sem("e_rows_set")
        idx_loaded, idx_again, w1_loaded, w2_loaded, bias_loaded, gathered, scattered = (
            twos(n) for n in ("idx_loaded", "idx_again", "w1_loaded", "w2_loaded", "bias_loaded", "gathered", "scattered"))
        turned, xhi, xlo = sem("e_turned"), sem("e_xhi"), sem("e_xlo")
        l1, gelu, ahi, alo, l2, ysummed, ydone, kept = (
            sem("e_" + n) for n in ("l1", "gelu", "ahi", "alo", "l2", "ysummed", "ydone", "kept"))

        turn_bank = psum[:, 0, :]
        l1_bank = [psum[:, 1 + k, :].rearrange("p (f t) -> p f t", f=2) for k in range(3)]
        l2_bank = [[psum[:, 4 + 2 * i + n, 0:2 * C].rearrange("p (a c) -> p a c", a=2) for n in range(2)]
                   for i in range(2)]

        def since(eng, s, tile, per, add):
            if tile.static:
                if per * tile.n + add > 0:
                    eng.wait_ge(s, per * tile.n + add)
            else:
                reg_wait(eng, s, tile.w * (2 * per) + (per * tile.p + add), eng.engine == mybir.EngineType.Pool)

        def landed(eng, s, tile, per, back=0):
            if tile.static:
                if tile.w + 1 - back > 0:
                    eng.wait_ge(s[tile.p], per * (tile.w + 1 - back))
            else:
                reg_wait(eng, s[tile.p], tile.w * per + per * (1 - back), eng.engine == mybir.EngineType.Pool)

        def run(eng, body):
            def pair(k):
                for p in range(2):
                    def tile(lag):
                        if isinstance(k, int) and 2 * k + p < lag:
                            return None
                        return Tile(k + (p - lag) // 2, (p - lag) % 2)
                    body(tile)
            for k in range(LAGS // 2 + 1):
                pair(k)
            count = eng.value_load(table[0:1, 3 * TABLE:3 * TABLE + 1], min_val=0, max_val=TABLE - 6)
            with eng.Fori(LAGS // 2 + 1, PAIRS) as k:
                with eng.If(k * 2 < count + (LAGS + 2)):
                    pair(k)
            return eng.value_load(table[0:1, 3 * TABLE + 1:3 * TABLE + 2], min_val=1, max_val=PAIRS)

        def entry(eng, tile, column, most):
            return eng.value_load(table[0:1, bass.ds(tile.n + column * TABLE, 1)], min_val=0, max_val=most)

        with nc.Block() as block:
            @block.sync
            def _(sp):
                def indices(tile, dst, free, done, back):
                    if tile is None:
                        return
                    landed(sp, free, tile, 32, back)
                    row = entry(sp, tile, 0, NULL_AT)
                    sp.dma_start(dst[tile.p][:], lists[bass.ds(row, TS)].rearrange("(p n) o -> p (n o)", n=2))\
                        .then_inc(done[tile.p], 16)

                def body(tile):
                    indices(tile(0), idx_in, gathered, idx_loaded, 1)
                    indices(tile(3), idx_out, scattered, idx_again, 1)
                more = run(sp, body)
                for i in range(2):
                    reg_wait(sp, idx_loaded[i], more * 16 + 32)
                    reg_wait(sp, w1_loaded[i], more * 16 + 16 * (2 - i))
                    reg_wait(sp, w2_loaded[i], more * 16 + 16 * (2 - i))
                    reg_wait(sp, bias_loaded[i], more * 32 + 32 * (2 - i))
                    reg_wait(sp, idx_again[i], more * 16 + 16 * (1 - i))

            @block.gpsimd
            def _(pool):
                for i in range(2):
                    pool.memset(rows[i][:], 0.0).then_inc(rows_set, 1)
                pool.wait_ge(rows_set, 2)

                def gather(tile):
                    if tile is None:
                        return
                    landed(pool, idx_loaded, tile, 16)
                    since(pool, turned, tile, 1, -1)
                    since(pool, kept, tile, 1, -1)
                    for n in range(2):
                        pool.indirect_dma_start(rows[tile.p][:, n, :], None, expert_in,
                                                bass.IndirectOffsetOnAxis(ap=idx_in[tile.p][:, n:n + 1], axis=0),
                                                bounds_check=NROW - 1, oob_is_err=False).then_inc(gathered[tile.p], 16)

                def scatter(tile):
                    if tile is None:
                        return
                    landed(pool, idx_again, tile, 16)
                    since(pool, ydone, tile, 1, 1)
                    before = Tile(tile.w - 1 + tile.p, 1 - tile.p)
                    landed(pool, scattered, before, 32)
                    for n in range(2):
                        pool.indirect_dma_start(out, bass.IndirectOffsetOnAxis(ap=idx_out[tile.p][:, n:n + 1], axis=0),
                                                y[tile.p][:, n, :], None, bounds_check=NROW - 1, oob_is_err=False,
                                                compute_op=ALU.add).then_inc(scattered[tile.p], 16)

                def place(tile):
                    if not tile.static:
                        with pool.If(tile.w * 2 < LEAST_C - tile.p):
                            place_two(tile)
                    elif tile.n < LEAST_C:
                        place_two(tile)

                def place_two(tile):
                    p = tile.p
                    landed(pool, placed, tile, 32, 1)
                    pool.tensor_copy(placing[p][:], place_id[1][:, bass.ds(tile.n * 2, 2), :]).then_inc(placing_set, 1)
                    since(pool, placing_set, tile, 1, 1)
                    for j in range(2):
                        pool.indirect_dma_start(all_lists[1],
                                                bass.IndirectOffsetOnAxis(ap=placing[p][:, j, 0:1], axis=0),
                                                placing[p][:, j, 1:2], None, bounds_check=LIST - 1,
                                                oob_is_err=False).then_inc(placed[p], 16)

                def body(tile):
                    gather(tile(0))
                    if which == 0:
                        place(tile(0))
                    scatter(tile(4))
                more = run(pool, body)
                for i in range(2):
                    reg_wait(pool, gathered[i], more * 32 + 64, True)
                    reg_wait(pool, scattered[i], more * 32, True)
                if which == 0:
                    for i in range(2):
                        pool.wait_ge(placed[i], 16 * SCATTERS // 2)
                pool.drain()

            @block.tensor
            def _(pe):
                def turn(tile):
                    if tile is None:
                        return
                    landed(pe, gathered, tile, 32)
                    since(pe, xlo, tile, 1, 0)
                    for n in range(2):
                        for c in range(2):
                            mm = pe.transpose(turn_bank[0:CH, c * TS + n * 128:c * TS + (n + 1) * 128],
                                              rows[tile.p][:, n, c * CH:(c + 1) * CH], identity[:])
                    mm.then_inc(turned, 1)

                def layer1(tile):
                    if tile is None:
                        return
                    since(pe, xlo, tile, 1, 1)
                    landed(pe, w1_loaded, tile, 16)
                    w, x_ = w1b[tile.p], [xt[a][tile.p] for a in range(2)]
                    for k in range(3):
                        since(pe, gelu, tile, 3, k - 2)
                        for i in range(2):
                            for c in range(2):
                                q, at = divmod((c * FT + 2 * k + i) * 128, WC)
                                f = slice(at, at + 128)
                                mm = split3(pe, l1_bank[k][:, i, :], w[:, q, 0, f], w[:, q, 1, f], x_[0][:, c, :],
                                            x_[1][:, c, :], c == 0, c == 1)
                        mm.then_inc(l1, 1)

                def layer2(tile):
                    if tile is None:
                        return
                    since(pe, ydone, tile, 1, -1)
                    landed(pe, w2_loaded, tile, 16)
                    p = tile.p
                    for f in range(FT):
                        if f % 2 == 0:
                            since(pe, alo, tile, 3, f // 2 + 1)
                        q, at = divmod(f * C, WC)
                        for n in range(2):
                            s = slice(n * 128, (n + 1) * 128)
                            pe.matmul(l2_bank[p][n], act_p[0][p][:, f, s], w2b[p][:, q, :, at:at + C],
                                      start=(f == 0), stop=False, skip_group_check=True)
                            mm = pe.matmul(l2_bank[p][n][:, 0, :], act_p[1][p][:, f, s], w2b[p][:, q, 0, at:at + C],
                                           start=False, stop=(f == FT - 1), skip_group_check=True)
                    mm.then_inc(l2, 1)

                def body(tile):
                    turn(tile(1))
                    layer2(tile(3))
                    layer1(tile(2))
                run(pe, body)

            @block.scalar
            def _(act):
                def weights1(tile):
                    if tile is None:
                        return
                    e, new, p = entry(act, tile, 1, ALL_E - 1), entry(act, tile, 2, 1) > 0, tile.p
                    since(act, l1, tile, 3, -3)
                    act.dma_start(w1b[p][:].bitcast(F32).rearrange("p q a n -> p q (a n)"),
                                 w_parts[bass.ds(e * QE, Q1), 0:CH].rearrange("q p n -> p q n"), cond=new)\
                        .then_inc(w1_loaded[p], 16)

                def weights2(tile):
                    if tile is None:
                        return
                    e, new, p = entry(act, tile, 1, ALL_E - 1), entry(act, tile, 2, 1) > 0, tile.p
                    since(act, l2, tile, 1, -1)
                    act.dma_start(w2b[p][:].bitcast(F32).rearrange("p q a n -> p q (a n)"),
                                 w_parts[bass.ds(e * QE + Q1, Q2)].rearrange("q p n -> p q n"), cond=new)\
                        .then_inc(w2_loaded[p], 16)

                def biases(tile):
                    if tile is None:
                        return
                    e, new, p = entry(act, tile, 1, ALL_E - 1), entry(act, tile, 2, 1) > 0, tile.p
                    since(act, ydone, tile, 1, -1)
                    act.dma_start(b1b[p][:], b1[bass.ds(e, 1)].rearrange("e p n -> (e p) n"), cond=new)\
                        .then_inc(bias_loaded[p], 16)
                    act.dma_start(b2b[p][:], b2[bass.ds(e, 1)].rearrange("e p n -> (e p) n"), cond=new)\
                        .then_inc(bias_loaded[p], 16)

                def x_hi(tile):
                    if tile is None:
                        return
                    since(act, turned, tile, 1, 1)
                    since(act, l1, tile, 3, -3)
                    act.copy(xt[0][tile.p][:].rearrange("p c t -> p (c t)"), turn_bank[0:CH, :]).then_inc(xhi, 1)

                def gelus(tile):
                    if tile is None:
                        return
                    since(act, alo, tile, 3, -3)
                    landed(act, bias_loaded, tile, 32)
                    for k in range(3):
                        since(act, l1, tile, 3, k + 1)
                        for i in range(2):
                            f = 2 * k + i
                            ins = act.activation(act_f[tile.p][:, f, :], l1_bank[k][:, i, :], ACT.Gelu,
                                                 bias=b1b[tile.p][:, f:f + 1])
                        ins.then_inc(gelu, 1)

                def body(tile):
                    weights1(tile(1))
                    x_hi(tile(1))
                    weights2(tile(1))
                    gelus(tile(2))
                    biases(tile(1))
                run(act, body)

            @block.vector
            def _(dve):
                def keep(tile):
                    if tile is None:
                        return
                    landed(dve, gathered, tile, 32)
                    since(dve, ydone, tile, 1, -1)
                    dve.tensor_copy(scale[tile.p][:], rows[tile.p][:, :, C + which]).then_inc(kept, 1)

                def x_lo(tile):
                    if tile is None:
                        return
                    since(dve, xhi, tile, 1, 1)
                    dve.tensor_tensor(xt[1][tile.p][:].rearrange("p c t -> p (c t)"), turn_bank[0:CH, :],
                                      xt[0][tile.p][:].bitcast(F32).rearrange("p c t -> p (c t)"), ALU.subtract)\
                        .then_inc(xlo, 1)

                def parts(tile):
                    if tile is None:
                        return
                    since(dve, l2, tile, 1, -1)
                    p = tile.p
                    for k in range(3):
                        since(dve, gelu, tile, 3, k + 1)
                        f = slice(2 * k, 2 * k + 2)
                        dve.tensor_copy(act_p[0][p][:, f, :], act_f[p][:, f, :]).then_inc(ahi, 1)
                        since(dve, ahi, tile, 3, k + 1)
                        dve.tensor_tensor(act_p[1][p][:, f, :], act_f[p][:, f, :], act_p[0][p][:, f, :].bitcast(F32),
                                          ALU.subtract).then_inc(alo, 1)

                def result(tile):
                    if tile is None:
                        return
                    since(dve, l2, tile, 1, 1)
                    landed(dve, bias_loaded, tile, 32)
                    landed(dve, scattered, tile, 32, 1)
                    p = tile.p
                    for n in range(2):
                        ins = dve.tensor_tensor(ysum[:, n, :], l2_bank[p][n][:, 1, :], b2b[p][:], ALU.add)
                    ins.then_inc(ysummed, 1)
                    since(dve, ysummed, tile, 2, 1)
                    for n in range(2):
                        ins = dve.tensor_tensor(ysum[:, n, :], l2_bank[p][n][:, 0, :], ysum[:, n, :], ALU.add)
                    ins.then_inc(ysummed, 1)
                    since(dve, ysummed, tile, 2, 2)
                    for n in range(2):
                        ins = dve.tensor_scalar(y[p][:, n, :], ysum[:, n, :], scale[p][:, n:n + 1], None, ALU.mult)
                    ins.then_inc(ydone, 1)

                def body(tile):
                    x_lo(tile(1))
                    result(tile(3))
                    keep(tile(1))
                    parts(tile(2))
                run(dve, body)


_DEVICE = [("x", (IMAGES, 128, KIN, ROWS)), ("w_emb", (128, KIN, C)), ("tok_rows", (T, 2, C)), ("pos", (T, 2, C)),
           ("gamma", (C,)), ("beta", (C,)), ("w_qk", (CH, 2, 2 * C)), ("w_v", (CH, 2, C)), ("w_proj", (CH, 2, C)),
           ("w_router", (CH, 2, ALL_E)), ("b_router", (ALL_E,)), ("cos", (T, 2, D)), ("sin", (T, 2, D)),
           ("ident", (128, 128)), ("tri", (T, 4, T)), ("lower", (T, T)), ("w_experts", (ALL_E * QE, 128, WC)),
           ("b1", (ALL_E, 128, FT)), ("b2", (ALL_E, 128, C)), ("valid", (T, 2))]


def _tiles(rows):
    return np.ascontiguousarray(rows.reshape(2, T, -1).transpose(1, 0, 2))


def _constants():
    i = np.arange(TOKENS, dtype=np.float32)[:, None]
    j = np.arange(C, dtype=np.float32)[None, :]
    angle = (i / np.power(np.float32(10000.0), np.floor(j / 2.0) * 2.0 / C)).astype(np.float32)
    pos = np.zeros((ROWS, C), np.float32)
    pos[:TOKENS] = np.where(np.arange(C)[None, :] % 2 == 0, np.sin(angle), np.cos(angle))
    inv = (1.0 / np.float32(10000.0) ** (np.arange(0, D, 2, dtype=np.float32) / D)).astype(np.float32)
    ang = np.arange(ROWS, dtype=np.float32)[:, None] * inv[None, :]
    cos = np.concatenate([np.cos(ang)] * 2, axis=1)
    sin = np.concatenate([-np.sin(ang), np.sin(ang)], axis=1)
    q = np.arange(T)
    tri = np.where(q[None, :] > q[:, None], -1e30, 0.0).astype(np.float32)
    valid = np.ones((T, 2), np.float32)
    valid[TOKENS - T:, 1] = 0.0
    return dict(pos=_tiles(pos), cos=_tiles(cos.astype(np.float32)), sin=_tiles(sin.astype(np.float32)),
                ident=np.eye(128, dtype=np.float32), tri=np.repeat(tri[:, None, :], 4, axis=1),
                lower=np.triu(np.ones((T, T), np.float32), 1), valid=valid)


def _halves(w):
    return np.ascontiguousarray(w.reshape(2, CH, -1).transpose(1, 0, 2))


def _layout(a):
    a = {k: np.asarray(v) for k, v in a.items()}
    img = a["x"].reshape(IMAGES, 3, PATCHES, PIX, PATCHES, PIX).transpose(0, 1, 3, 5, 2, 4)
    img = img.reshape(IMAGES, KIN, 128, PATCHES * PATCHES)
    x = np.zeros((IMAGES, 128, KIN, ROWS), np.float32)
    x[..., 1:TOKENS] = img.transpose(0, 2, 1, 3)
    rows = np.empty((ROWS, C), np.float32)
    rows[:] = a["L0_tok_b"]
    rows[0] = a["L0_tok_class_token"][0]
    w_qkv = a["L0_attn_w_qkv"]
    w1 = np.concatenate([a["L0_ffn_W1c"], a["L0_ffn_W1u"]])
    w2 = np.concatenate([a["L0_ffn_W2c"], a["L0_ffn_W2u"]])
    b1 = np.concatenate([a["L0_ffn_b1c"], a["L0_ffn_b1u"]])
    b2 = np.concatenate([a["L0_ffn_b2c"], a["L0_ffn_b2u"]])
    w_experts = np.zeros((ALL_E, QE, 128, WC), np.float32)
    w1 = w1.reshape(ALL_E, 2, CH, HID).transpose(0, 2, 1, 3).reshape(ALL_E, CH, Q1, WC)
    w2 = w2.reshape(ALL_E, FT, 128, C).transpose(0, 2, 1, 3).reshape(ALL_E, 128, Q2, WC)
    w_experts[:, :Q1, :CH] = w1.transpose(0, 2, 1, 3)
    w_experts[:, Q1:] = w2.transpose(0, 2, 1, 3)
    return dict(
        _constants(), x=x, w_emb=a["L0_tok_W"].T.reshape(KIN, 128, C).transpose(1, 0, 2), tok_rows=_tiles(rows),
        gamma=a["L0_tok_gamma"], beta=a["L0_tok_beta"], w_qk=_halves(w_qkv[:2 * C].T), w_v=_halves(w_qkv[2 * C:].T),
        w_proj=_halves(a["L0_attn_w_proj"].T),
        w_router=_halves(np.concatenate([a["L0_ffn_Wsc"], a["L0_ffn_Wsu"]], axis=1)),
        b_router=np.concatenate([a["L0_ffn_bsc"], a["L0_ffn_bsu"]]),
        w_experts=w_experts.reshape(ALL_E * QE, 128, WC),
        b1=b1.reshape(ALL_E, FT, 128).transpose(0, 2, 1), b2=np.repeat(b2[:, None, :], 128, axis=1))


def kernel(**inputs):
    import concourse.bacc as bacc
    from concourse.bass_utils import run_bass_kernel_spmd

    nc = bacc.Bacc("TRN2", target_bir_lowering=False, num_devices=1)
    given = _layout(inputs)
    arrays, args = {}, []
    for name, shape in _DEVICE:
        a = np.ascontiguousarray(given[name])
        assert a.shape == shape, (name, a.shape)
        arrays[f"in_{name}"] = a
        args.append(nc.dram_tensor(f"in_{name}", shape, mybir.dt.from_np(a.dtype), kind="ExternalInput").ap())
    args.append(nc.dram_tensor("out_rows", (NROW, C), F32, kind="ExternalOutput").ap())
    program(nc, *args)
    r = run_bass_kernel_spmd(nc, [arrays], core_ids=[0])
    got = r.results[0]["out_rows"]
    return np.ascontiguousarray(got.reshape(IMAGES, ROWS, C)[:, :TOKENS])
```
